# Optimizing a Trainium2 kernel written in Bass

```python
import numpy as np
import jax
import jax.numpy as jnp

def _softmax(x, axis=-1):
    return jax.nn.softmax(x, axis=axis)

def _gelu(x):
    return jax.nn.gelu(x, approximate=True)

def _silu(x):
    return jax.nn.silu(x)

def _sigmoid(x):
    return jax.nn.sigmoid(x)

def _layernorm(x, axis=-1, eps=1e-05):
    m = jnp.mean(x, axis=axis, keepdims=True)
    v = jnp.var(x, axis=axis, keepdims=True)
    return (x - m) / jnp.sqrt(v + eps)

def _scatter_add(tgt, idx, src, axis=0):
    return tgt.at[idx].add(src)

def _segment_sum(src, seg, n):
    return jax.ops.segment_sum(src, seg, n)
kernel_name = 'mk_seq_preln_d1_jaxref_r8_227589'

def setup_inputs(seed: int=0):
    np.random.seed(seed)
    _w = jnp.asarray

    def _L0_attn_setup():
        import jax, jax.numpy as jnp
        import numpy as np
        DIM = 128
        HEADS = 16
        HEAD_DIM = DIM // HEADS

        def apply_rope(x):
            B, S, H, D = x.shape
            half = D // 2
            freqs = 1.0 / 10000.0 ** (jnp.arange(half, dtype=jnp.float32) / half)
            pos = jnp.arange(S, dtype=jnp.float32)
            angles = pos[:, None] * freqs[None, :]
            sin = jnp.sin(angles)[None, :, None, :]
            cos = jnp.cos(angles)[None, :, None, :]
            x1, x2 = (x[..., :half], x[..., half:])
            return jnp.concatenate([x1 * cos - x2 * sin, x1 * sin + x2 * cos], axis=-1)
        key = jax.random.key(seed)
        ks = jax.random.split(key, 5)
        x = jax.random.normal(ks[0], (2, 256, DIM), dtype=jnp.float32)
        s = 1.0 / np.sqrt(DIM)
        qkv_w = jax.random.uniform(ks[1], (3 * DIM, DIM), minval=-s, maxval=s, dtype=jnp.float32)
        qkv_b = jax.random.uniform(ks[2], (3 * DIM,), minval=-s, maxval=s, dtype=jnp.float32)
        proj_w = jax.random.uniform(ks[3], (DIM, DIM), minval=-s, maxval=s, dtype=jnp.float32)
        proj_b = jax.random.uniform(ks[4], (DIM,), minval=-s, maxval=s, dtype=jnp.float32)
        return {'x': x, 'qkv_w': qkv_w, 'qkv_b': qkv_b, 'proj_w': proj_w, 'proj_b': proj_b}
    _L0_attn_in = _L0_attn_setup()

    def _L0_ffn_setup():
        import jax, jax.numpy as jnp
        import numpy as np
        DIM = 128
        DEPTH = 6
        HEADS = 16
        DIM_HEAD = 64
        WINDOW = 32
        INNER = HEADS * DIM_HEAD
        DIM_INNER = int(DIM * 4 * 2 / 3)
        QK_SCALE = 8.0

        def shift_tokens(t):
            a, s = jnp.split(t, 2, -1)
            s = jnp.pad(s, ((0, 0), (1, 0), (0, 0)))[:, :-1]
            return jnp.concatenate([a, s], -1)

        def l2norm(t):
            return t / jnp.maximum(jnp.linalg.norm(t, axis=-1, keepdims=True), 1e-12)

        def rotate_half(x):
            x1, x2 = jnp.split(x, 2, -1)
            return jnp.concatenate([-x2, x1], -1)

        def rotary_tables(n):
            half = jnp.arange(0, DIM_HEAD, 2, dtype=jnp.float32)
            inv_freq = 1.0 / 10000.0 ** (half / DIM_HEAD)
            t = jnp.arange(n, dtype=jnp.float32)
            freqs = t[:, None] * inv_freq[None, :]
            freqs = jnp.concatenate([freqs, freqs], -1)
            base_scale = (half + 0.4 * DIM_HEAD) / (1.4 * DIM_HEAD)
            power = (t - n // 2) / (WINDOW // 2)
            scale = base_scale[None, :] ** power[:, None]
            scale = jnp.concatenate([scale, scale], -1)
            return (freqs, scale)

        def local_attention(q, k, v):
            b, h, n, d = q.shape
            w = WINDOW
            nw = n // w
            bq = q.reshape(b, h, nw, w, d)
            bk = k.reshape(b, h, nw, w, d)
            bv = v.reshape(b, h, nw, w, d)

            def look(t):
                p = jnp.pad(t, ((0, 0), (0, 0), (1, 0), (0, 0), (0, 0)))
                return jnp.concatenate([p[:, :, :nw], p[:, :, 1:]], axis=3)
            bk2, bv2 = (look(bk), look(bv))
            seq = jnp.arange(n).reshape(nw, w)
            seq_p = jnp.pad(seq, ((1, 0), (0, 0)), constant_values=-1)
            jt = jnp.concatenate([seq_p[:nw], seq_p[1:]], axis=1)
            it = seq[:, :, None]
            jb = jt[:, None, :]
            mask = (it < jb) | (it > jb + w) | (jb == -1)
            sim = jnp.einsum('bhwie,bhwje->bhwij', bq, bk2) * QK_SCALE
            sim = jnp.where(mask, -jnp.finfo(sim.dtype).max, sim)
            attn = jax.nn.softmax(sim, -1)
            out = jnp.einsum('bhwij,bhwje->bhwie', attn, bv2)
            return out.reshape(b, h, n, d)

        def attn_layer(x, Wqkv, qs, ksc, Wo):
            b, n, _ = x.shape
            qkv = x @ Wqkv
            q, k, v = jnp.split(qkv, 3, -1)
            sh = lambda t: t.reshape(b, n, HEADS, DIM_HEAD).transpose(0, 2, 1, 3)
            q, k, v = (sh(q), sh(k), sh(v))
            q = l2norm(q) * qs
            k = l2norm(k) * ksc
            freqs, scale = rotary_tables(n)
            cos, sin = (jnp.cos(freqs), jnp.sin(freqs))
            q = q * cos * scale + rotate_half(q) * sin * scale
            inv = 1.0 / scale
            k = k * cos * inv + rotate_half(k) * sin * inv
            out = local_attention(q, k, v)
            out = out.transpose(0, 2, 1, 3).reshape(b, n, INNER)
            return out @ Wo

        def ffn_layer(x, g, bln, W1, b1, W2, b2):
            mu = x.mean(-1, keepdims=True)
            var = ((x - mu) ** 2).mean(-1, keepdims=True)
            xn = (x - mu) / jnp.sqrt(var + 1e-05) * g + bln
            hg = xn @ W1 + b1
            a, gate = jnp.split(hg, 2, -1)
            return a * jax.nn.gelu(gate, approximate=False) @ W2 + b2
        key = jax.random.key(seed)
        ks = jax.random.split(key, 8)
        B, N = (2, 256)
        init = lambda k, shape: jax.random.normal(k, shape, jnp.float32) * 0.02
        return {'x': jax.random.normal(ks[0], (B, N, DIM), jnp.float32), 'Wqkv': init(ks[1], (DEPTH, DIM, 3 * INNER)), 'q_scale': jnp.ones((DEPTH, DIM_HEAD), jnp.float32), 'k_scale': jnp.ones((DEPTH, DIM_HEAD), jnp.float32), 'Wo': init(ks[2], (DEPTH, INNER, DIM)), 'ln_g': jnp.ones((DEPTH, DIM), jnp.float32), 'ln_b': jnp.zeros((DEPTH, DIM), jnp.float32), 'W1': init(ks[3], (DEPTH, DIM, 2 * DIM_INNER)), 'b1': jnp.zeros((DEPTH, 2 * DIM_INNER), jnp.float32), 'W2': init(ks[4], (DEPTH, DIM_INNER, DIM)), 'b2': jnp.zeros((DEPTH, DIM), jnp.float32)}
    _L0_ffn_in = _L0_ffn_setup()
    _d = {'L0_attn_x': _L0_attn_in['x'], 'L0_attn_qkv_w': _L0_attn_in['qkv_w'], 'L0_attn_qkv_b': _L0_attn_in['qkv_b'], 'L0_attn_proj_w': _L0_attn_in['proj_w'], 'L0_attn_proj_b': _L0_attn_in['proj_b'], 'L0_ffn_Wqkv': _L0_ffn_in['Wqkv'], 'L0_ffn_q_scale': _L0_ffn_in['q_scale'], 'L0_ffn_k_scale': _L0_ffn_in['k_scale'], 'L0_ffn_Wo': _L0_ffn_in['Wo'], 'L0_ffn_ln_g': _L0_ffn_in['ln_g'], 'L0_ffn_ln_b': _L0_ffn_in['ln_b'], 'L0_ffn_W1': _L0_ffn_in['W1'], 'L0_ffn_b1': _L0_ffn_in['b1'], 'L0_ffn_W2': _L0_ffn_in['W2'], 'L0_ffn_b2': _L0_ffn_in['b2']}
    _x0 = _d['L0_attn_x']
    _d['L0_attn_x'] = jax.random.normal(jax.random.fold_in(jax.random.key(seed), 1), (8, 512, 128), dtype=_x0.dtype)
    del _x0
    return _d

def reference(L0_attn_x, L0_attn_qkv_w, L0_attn_qkv_b, L0_attn_proj_w, L0_attn_proj_b, L0_ffn_Wqkv, L0_ffn_q_scale, L0_ffn_k_scale, L0_ffn_Wo, L0_ffn_ln_g, L0_ffn_ln_b, L0_ffn_W1, L0_ffn_b1, L0_ffn_W2, L0_ffn_b2):

    def _L0_attn_ref(x, qkv_w, qkv_b, proj_w, proj_b):
        import jax, jax.numpy as jnp
        import numpy as np
        DIM = 128
        HEADS = 16
        HEAD_DIM = DIM // HEADS

        def apply_rope(x):
            B, S, H, D = x.shape
            half = D // 2
            freqs = 1.0 / 10000.0 ** (jnp.arange(half, dtype=jnp.float32) / half)
            pos = jnp.arange(S, dtype=jnp.float32)
            angles = pos[:, None] * freqs[None, :]
            sin = jnp.sin(angles)[None, :, None, :]
            cos = jnp.cos(angles)[None, :, None, :]
            x1, x2 = (x[..., :half], x[..., half:])
            return jnp.concatenate([x1 * cos - x2 * sin, x1 * sin + x2 * cos], axis=-1)
        B, S, D = x.shape
        qkv = x @ qkv_w.T + qkv_b
        q, k, v = jnp.split(qkv, 3, axis=-1)
        q = q.reshape(B, S, HEADS, HEAD_DIM)
        k = k.reshape(B, S, HEADS, HEAD_DIM)
        v = v.reshape(B, S, HEADS, HEAD_DIM)
        q = apply_rope(q)
        k = apply_rope(k)
        scale = 1.0 / np.sqrt(HEAD_DIM)
        attn = jnp.einsum('bqhd,bkhd->bhqk', q, k) * scale
        mask = jnp.triu(jnp.ones((S, S), dtype=bool), k=1)
        attn = jnp.where(mask[None, None], -1000000000.0, attn)
        attn = jax.nn.softmax(attn, axis=-1)
        out = jnp.einsum('bhqk,bkhd->bqhd', attn, v).reshape(B, S, D)
        return out @ proj_w.T + proj_b

    def _L0_ffn_ref(x, Wqkv, q_scale, k_scale, Wo, ln_g, ln_b, W1, b1, W2, b2):
        import jax, jax.numpy as jnp
        import numpy as np
        DIM = 128
        DEPTH = 6
        HEADS = 16
        DIM_HEAD = 64
        WINDOW = 32
        INNER = HEADS * DIM_HEAD
        DIM_INNER = int(DIM * 4 * 2 / 3)
        QK_SCALE = 8.0

        def shift_tokens(t):
            a, s = jnp.split(t, 2, -1)
            s = jnp.pad(s, ((0, 0), (1, 0), (0, 0)))[:, :-1]
            return jnp.concatenate([a, s], -1)

        def l2norm(t):
            return t / jnp.maximum(jnp.linalg.norm(t, axis=-1, keepdims=True), 1e-12)

        def rotate_half(x):
            x1, x2 = jnp.split(x, 2, -1)
            return jnp.concatenate([-x2, x1], -1)

        def rotary_tables(n):
            half = jnp.arange(0, DIM_HEAD, 2, dtype=jnp.float32)
            inv_freq = 1.0 / 10000.0 ** (half / DIM_HEAD)
            t = jnp.arange(n, dtype=jnp.float32)
            freqs = t[:, None] * inv_freq[None, :]
            freqs = jnp.concatenate([freqs, freqs], -1)
            base_scale = (half + 0.4 * DIM_HEAD) / (1.4 * DIM_HEAD)
            power = (t - n // 2) / (WINDOW // 2)
            scale = base_scale[None, :] ** power[:, None]
            scale = jnp.concatenate([scale, scale], -1)
            return (freqs, scale)

        def local_attention(q, k, v):
            b, h, n, d = q.shape
            w = WINDOW
            nw = n // w
            bq = q.reshape(b, h, nw, w, d)
            bk = k.reshape(b, h, nw, w, d)
            bv = v.reshape(b, h, nw, w, d)

            def look(t):
                p = jnp.pad(t, ((0, 0), (0, 0), (1, 0), (0, 0), (0, 0)))
                return jnp.concatenate([p[:, :, :nw], p[:, :, 1:]], axis=3)
            bk2, bv2 = (look(bk), look(bv))
            seq = jnp.arange(n).reshape(nw, w)
            seq_p = jnp.pad(seq, ((1, 0), (0, 0)), constant_values=-1)
            jt = jnp.concatenate([seq_p[:nw], seq_p[1:]], axis=1)
            it = seq[:, :, None]
            jb = jt[:, None, :]
            mask = (it < jb) | (it > jb + w) | (jb == -1)
            sim = jnp.einsum('bhwie,bhwje->bhwij', bq, bk2) * QK_SCALE
            sim = jnp.where(mask, -jnp.finfo(sim.dtype).max, sim)
            attn = jax.nn.softmax(sim, -1)
            out = jnp.einsum('bhwij,bhwje->bhwie', attn, bv2)
            return out.reshape(b, h, n, d)

        def attn_layer(x, Wqkv, qs, ksc, Wo):
            b, n, _ = x.shape
            qkv = x @ Wqkv
            q, k, v = jnp.split(qkv, 3, -1)
            sh = lambda t: t.reshape(b, n, HEADS, DIM_HEAD).transpose(0, 2, 1, 3)
            q, k, v = (sh(q), sh(k), sh(v))
            q = l2norm(q) * qs
            k = l2norm(k) * ksc
            freqs, scale = rotary_tables(n)
            cos, sin = (jnp.cos(freqs), jnp.sin(freqs))
            q = q * cos * scale + rotate_half(q) * sin * scale
            inv = 1.0 / scale
            k = k * cos * inv + rotate_half(k) * sin * inv
            out = local_attention(q, k, v)
            out = out.transpose(0, 2, 1, 3).reshape(b, n, INNER)
            return out @ Wo

        def ffn_layer(x, g, bln, W1, b1, W2, b2):
            mu = x.mean(-1, keepdims=True)
            var = ((x - mu) ** 2).mean(-1, keepdims=True)
            xn = (x - mu) / jnp.sqrt(var + 1e-05) * g + bln
            hg = xn @ W1 + b1
            a, gate = jnp.split(hg, 2, -1)
            return a * jax.nn.gelu(gate, approximate=False) @ W2 + b2
        for i in range(DEPTH):
            x = attn_layer(shift_tokens(x), Wqkv[i], q_scale[i], k_scale[i], Wo[i]) + x
            x = ffn_layer(shift_tokens(x), ln_g[i], ln_b[i], W1[i], b1[i], W2[i], b2[i]) + x
        return x
    x = L0_attn_x
    x = x + _L0_attn_ref(_layernorm(x, axis=-1), L0_attn_qkv_w, L0_attn_qkv_b, L0_attn_proj_w, L0_attn_proj_b)
    x = x + _L0_ffn_ref(_layernorm(x, axis=-1), L0_ffn_Wqkv, L0_ffn_q_scale, L0_ffn_k_scale, L0_ffn_Wo, L0_ffn_ln_g, L0_ffn_ln_b, L0_ffn_W1, L0_ffn_b1, L0_ffn_W2, L0_ffn_b2)
    return x

_drawn_inputs = setup_inputs


def setup_inputs(seed=0):
    import zlib

    import numpy as np

    out = dict(_drawn_inputs(seed))
    spreads = {'L0_ffn_q_scale': (1.0, 0.6),
     'L0_ffn_k_scale': (1.0, 0.6),
     'L0_ffn_ln_g': (1.0, 0.6),
     'L0_ffn_ln_b': (0.0, 0.8),
     'L0_ffn_b1': (0.0, 0.8),
     'L0_ffn_b2': (0.0, 0.1)}
    factors = {'L0_ffn_W1': 3.646, 'L0_ffn_W2': 3.58}
    for name, (base, spread) in spreads.items():
        noise = np.random.default_rng([zlib.crc32(name.encode()), seed]).standard_normal(out[name].shape)
        drawn = base * np.exp(spread * noise) if base else spread * noise
        out[name] = jnp.asarray(drawn.astype(out[name].dtype))
    for name, factor in factors.items():
        out[name] = (out[name] * factor).astype(out[name].dtype)
    return out
```

```python
import numpy as np
import concourse.bass as bass
from concourse import mybir
from contextlib import ExitStack

F32 = mybir.dt.float32
BF16 = mybir.dt.bfloat16
ALU = mybir.AluOpType
ACT = mybir.ActivationFunctionType
AX = mybir.AxisListType

D = 128
B = 8
S = 512
T = S // 128
HEADS = 16
LAYERS = 6

HD = D // HEADS
A_SCALE = 1.0 / float(np.sqrt(HD))
VROW = HEADS * (128 + HD)

WD = 64
INNER = HEADS * WD
WIN = 32
HALF = 8
STEPS = 2 * T
QK_SCALE = 8.0
MASKED = -1.0e30

FF = 341
FC = [128, 128, FF - 256]
EPS = 1e-5
NVEC = 9


def flat(ap):
    return ap.rearrange("p a b -> p (a b)")


def program(nc, xT, a_wT, a_b, a_pT, a_pb, a_rope, win_rope, masks, ident_in,
            wqkv, wo, w1, w2, vecs, qk_scale, outT):
    ctx = ExitStack()
    with ctx:
        def sem(name):
            return ctx.enter_context(nc.semaphore(name))

        def sb(stack, name, shape, dt=F32):
            return stack.enter_context(nc.sbuf_tensor(name, shape, dt))

        def ps(stack, name, shape, dt=F32):
            return stack.enter_context(nc.psum_tensor(name, shape, dt))

        x1 = sb(ctx, "x1", [128, B, S])
        xres = sb(ctx, "xres", [128, B, S])
        xn = sb(ctx, "xn", [128, B, S])
        ident = sb(ctx, "ident", [128, 128])
        ident_bf = sb(ctx, "ident_bf", [128, 128], BF16)
        mean_w = sb(ctx, "mean_w", [128, 128])
        eps_col = sb(ctx, "eps_col", [128, 1])
        mask_bf = sb(ctx, "mask_bf", [128, 128 + 2 * 256], BF16)
        ln_x = sb(ctx, "ln_x", [128, 2, S])
        ln_c = sb(ctx, "ln_c", [128, 2, S])
        ln_sq = sb(ctx, "ln_sq", [128, 2, S])
        ln_std = sb(ctx, "ln_std", [128, 2, S])
        ln_r = ln_sq
        ln_n = ln_std

        const_in = sem("const_in")
        waited = sem("waited")
        const_ready = sem("const_ready")
        x_in = sem("x_in")
        ln_x_ready = sem("ln_x_ready")
        ln_mean_ready = sem("ln_mean_ready")
        ln_c_ready = sem("ln_c_ready")
        ln_sq_ready = sem("ln_sq_ready")
        ln_var_ready = sem("ln_var_ready")
        ln_std_ready = sem("ln_std_ready")
        ln_r_ready = sem("ln_r_ready")
        ln_n_ready = sem("ln_n_ready")
        ln_done = sem("ln_done")

        def alone(engine):
            engine.sem_inc(waited, 1)

        def ln_scalar(act, src, b0, v, shift):
            for k in range(2):
                if shift:
                    act.activation(ln_x[0:64, k, :], src[0:64, b0 + k, :], ACT.Copy)
                    act.activation(ln_x[64:128, k, 1:S], src[64:128, b0 + k, 0:S - 1], ACT.Copy).then_inc(ln_x_ready, 1)
                else:
                    act.activation(ln_x[:, k, :], src[:, b0 + k, :], ACT.Copy).then_inc(ln_x_ready, 1)
            for k in range(2):
                act.wait_ge(ln_c_ready, v + k + 1)
                act.activation(ln_sq[:, k, :], ln_c[:, k, :], ACT.Square).then_inc(ln_sq_ready, 1)
            for k in range(2):
                act.wait_ge(ln_var_ready, v + k + 1)
                act.activation(ln_std[:, k, :], ln_bank[2 + k], ACT.Sqrt, bias=eps_col[:, :]).then_inc(ln_std_ready, 1)

        def ln_tensor(pe, v):
            for k in range(2):
                pe.wait_ge(ln_x_ready, v + k + 1)
                nc.tensor.matmul(ln_bank[k], mean_w[:, :], ln_x[:, k, :], start=True, stop=True).then_inc(ln_mean_ready, 1)
            for k in range(2):
                pe.wait_ge(ln_sq_ready, v + k + 1)
                nc.tensor.matmul(ln_bank[2 + k], mean_w[:, :], ln_sq[:, k, :], start=True, stop=True).then_inc(ln_var_ready, 1)

        def ln_vector(dve, dst, b0, v, gain=None, bias=None):
            for k in range(2):
                dve.wait_ge(ln_mean_ready, v + k + 1)
                dve.tensor_tensor(ln_c[:, k, :], ln_x[:, k, :], ln_bank[k], ALU.subtract).then_inc(ln_c_ready, 1)
            for k in range(2):
                dve.wait_ge(ln_std_ready, v + k + 1)
                dve.reciprocal(ln_r[:, k, :], ln_std[:, k, :]).then_inc(ln_r_ready, 1)
            for k in range(2):
                dve.wait_ge(ln_r_ready, v + k + 1)
                if gain is None:
                    dve.tensor_tensor(dst[:, b0 + k, :], ln_c[:, k, :], ln_r[:, k, :], ALU.mult).then_inc(ln_done, 1)
                else:
                    dve.tensor_tensor(ln_n[:, k, :], ln_c[:, k, :], ln_r[:, k, :], ALU.mult).then_inc(ln_n_ready, 1)
            if gain is not None:
                for k in range(2):
                    dve.wait_ge(ln_n_ready, v + k + 1 - 2 * B)
                    dve.tensor_scalar(dst[:, b0 + k, :], ln_n[:, k, :], gain, bias, ALU.mult, ALU.add).then_inc(ln_done, 1)
            dve.wait_ge(ln_done, v + 2)
            alone(dve)

        part = ExitStack()
        mask_f = sb(part, "mask_f", [128, 128 + 2 * 256])
        w_qkv_a = sb(part, "w_qkv_a", [128, 3 * D])
        bias_a = sb(part, "bias_a", [128, 3 * D])
        w_proj_a = sb(part, "w_proj_a", [128, D])
        bias_proj = sb(part, "bias_proj", [128, 1])
        rope_a = sb(part, "rope_a", [128, T, 2, HD])
        xa = sb(part, "xa", [128, S])
        qkv_a = sb(part, "qkv_a", [128, T, 3 * D])
        rot_a = sb(part, "rot_a", [128, T, 2 * D])
        rot_b = sb(part, "rot_b", [128, T, 2 * D])
        qk_pad = sb(part, "qk_pad", [128, T, 2 * HEADS, 32])
        v_pad = sb(part, "v_pad", [128, T, VROW])
        qT_a = sb(part, "qT_a", [128, 4, S])
        kT_a = sb(part, "kT_a", [128, 4, S])
        p_a = sb(part, "p_a", [128, 4, S])
        pn_a = sb(part, "pn_a", [128, 4, S])
        pT_a = sb(part, "pT_a", [128, 2, S])
        st_a = sb(part, "st_a", [128, 4, 4])
        ao_a = sb(part, "ao_a", [128, S])
        sc_psum = ps(part, "sc_psum", [128, 4, S])
        tr_psum = ps(part, "tr_psum", [128, 2, S])
        o_psum = ps(part, "o_psum", [128, S])
        m_psum = ps(part, "m_psum", [128, S])
        ln_bank = [sc_psum[:, k, :] for k in range(4)]

        a_x = sem("a_x")
        a_proj = sem("a_proj")
        a_qkv = sem("a_qkv")
        a_rota = sem("a_rota")
        a_rotb = sem("a_rotb")
        a_pad = sem("a_pad")
        a_vpad = sem("a_vpad")
        a_tr = sem("a_tr")
        a_trc = sem("a_trc")
        a_sc = sem("a_sc")
        a_max = sem("a_max")
        a_nmax = sem("a_nmax")
        a_exp = sem("a_exp")
        a_rec = sem("a_rec")
        a_pn = sem("a_pn")
        a_pt = sem("a_pt")
        a_ptc_act = sem("a_ptc_act")
        a_ptc_dve = sem("a_ptc_dve")
        a_pv = sem("a_pv")
        a_oc = sem("a_oc")
        a_out = sem("a_out")
        a_done = sem("a_done")

        G = 4 * T

        with nc.Block() as block:
            @block.sync
            def _(sp):
                sp.dma_start(x1[:, :, :], xT).then_inc(x_in, 16)
                sp.dma_start(ident[:, :], ident_in).then_inc(const_in, 16)
                sp.dma_start(mask_f[:, :], masks).then_inc(const_in, 16)
                sp.dma_start(w_qkv_a[:, :], a_wT).then_inc(const_in, 16)
                sp.dma_start(bias_a[:, :], a_b.partition_broadcast(128)).then_inc(const_in, 16)
                sp.dma_start(w_proj_a[:, :], a_pT).then_inc(const_in, 16)
                sp.dma_start(bias_proj[:, :], a_pb).then_inc(const_in, 16)
                sp.dma_start(rope_a[:, :, :, :], a_rope).then_inc(const_in, 16)

            @block.gpsimd
            def _(pool):
                pool.memset(mean_w[:, :], 1.0 / D).then_inc(const_ready, 1)
                pool.memset(eps_col[:, :], EPS).then_inc(const_ready, 1)
                pool.memset(v_pad[:, :, :], 0.0).then_inc(const_ready, 1)
                pool.memset(qk_pad[:, :, :, :], 0.0).then_inc(const_ready, 1)
                pool.wait_ge(const_in, 7 * 16)
                pool.tensor_copy(ident_bf[:, :], ident[:, :]).then_inc(const_ready, 1)
                pool.tensor_copy(mask_bf[:, :], mask_f[:, :]).then_inc(const_ready, 1)

            @block.scalar
            def _(act):
                act.wait_ge(x_in, 16)
                act.wait_ge(const_ready, 6)
                with act.Fori(0, B // 2) as pair:
                    b0 = pair * 2
                    ln_scalar(act, x1, b0, b0, False)
                act.wait_ge(ln_done, B)
                with act.Fori(0, B) as b:
                    act.activation(xa[:, :], xn[:, b, :], ACT.Copy).then_inc(a_x, 1)
                    for n in range(8):
                        act.wait_ge(a_tr, b * 8 + n + 1)
                        dst = (qT_a, kT_a)[n // 4]
                        act.activation(dst[:, n % 4, :], tr_psum[:, n % 2, :], ACT.Copy).then_inc(a_trc, 1)

                    def exponentials(g):
                        n = (g // 4 + 1) * 128
                        act.wait_ge(a_nmax, b * G + g + 1)
                        for h in range(4):
                            act.activation(p_a[:, h, 0:n], sc_psum[:, h, 0:n], ACT.Exp, bias=st_a[:, 1, h:h + 1],
                                           scale=A_SCALE, accum_out=st_a[:, 2, h:h + 1]).then_inc(a_exp, 1)

                    exponentials(0)
                    for g in range(G):
                        j, n = g // 4, (g // 4 + 1) * 128
                        if g + 1 < G:
                            exponentials(g + 1)
                        for h in (0, 2):
                            act.wait_ge(a_pt, (b * G + g) * 4 + h + 1)
                            act.activation(pT_a[:, 0, 0:n], tr_psum[:, 0, 0:n], ACT.Copy).then_inc(a_ptc_act, 1)
                        if g % 4 == 3:
                            act.wait_ge(a_pv, (b * G + g) * 4 + 4)
                            act.activation(ao_a[:, 128 * j:128 * j + 128], o_psum[:, 0:128], ACT.Copy).then_inc(a_oc, 1)
                act.wait_ge(a_done, B + 1)
                with act.Fori(0, B // 2) as pair:
                    b0 = pair * 2
                    ln_scalar(act, x1, b0, b0 + B, False)

            @block.tensor
            def _(pe):
                pe.wait_ge(const_in, 7 * 16)
                pe.wait_ge(const_ready, 6)
                with pe.Fori(0, B // 2) as pair:
                    b0 = pair * 2
                    ln_tensor(pe, b0)
                pe.wait_ge(ln_done, B)
                with pe.Fori(0, B) as b:
                    pe.wait_ge(a_x, b + 1)
                    for j in range(T):
                        if j == 0:
                            pe.wait_ge(a_done, b + 1)
                        else:
                            pe.wait_ge(a_qkv, b * T + j)
                        nc.tensor.matmul(m_psum[:, 0:3 * D], xa[:, 128 * j:128 * j + 128], w_qkv_a[:, :],
                                         start=True, stop=True).then_inc(a_proj, 1)
                    pe.wait_ge(a_pad, b + 1)
                    for n in range(8):
                        if n >= 2:
                            pe.wait_ge(a_trc, b * 8 + n - 1)
                        for j in range(T):
                            ins = nc.tensor.transpose(tr_psum[:, n % 2, 128 * j:128 * j + 128],
                                                      qk_pad[:, j, 4 * n:4 * n + 4, :], ident[:, :])
                        ins.then_inc(a_tr, 1)
                    pe.wait_ge(a_trc, b * 8 + 8)
                    pe.wait_ge(a_vpad, b + 1)

                    def scores(g):
                        j, c = g // 4, g % 4
                        n = 128 * (j + 1)
                        if g:
                            pe.wait_ge(a_exp, b * 4 * G + 4 * g)
                        for h in range(4):
                            r = slice(32 * h, 32 * h + 32)
                            nc.tensor.matmul(sc_psum[:, h, 0:n], qT_a[r, c, 128 * j:128 * j + 128], kT_a[r, c, 0:n],
                                             start=True, stop=False)
                        for h in range(4):
                            ins = nc.tensor.matmul(sc_psum[:, h, n - 128:n], ident_bf[:, :], mask_bf[:, 0:128],
                                                   start=False, stop=True)
                        ins.then_inc(a_sc, 1)

                    scores(0)
                    for g in range(G):
                        j, c = g // 4, g % 4
                        if g + 1 < G:
                            scores(g + 1)
                        pe.wait_ge(a_pn, b * G + g + 1)

                        def values(h):
                            if h % 2 == 0:
                                pe.wait_ge(a_ptc_act, (b * G + g) * 2 + h // 2 + 1)
                            else:
                                pe.wait_ge(a_ptc_dve, (b * G + g) * 2 + h // 2 + 1)
                            if c == 0 and h == 0 and j > 0:
                                pe.wait_ge(a_oc, b * T + j)
                            head = 4 * c + h
                            for k in range(j + 1):
                                ins = nc.tensor.matmul(o_psum[:, 0:128], v_pad[:, k, 128 * head:128 * head + 128],
                                                       pT_a[:, h % 2, 128 * k:128 * k + 128],
                                                       start=head == 0 and k == 0, stop=head == HEADS - 1 and k == j)
                            ins.then_inc(a_pv, 1)

                        for h in range(4):
                            if h >= 2:
                                values(h - 2)
                            for k in range(j + 1):
                                ins = nc.tensor.transpose(tr_psum[:, h % 2, 128 * k:128 * k + 128],
                                                          pn_a[:, h, 128 * k:128 * k + 128], ident[:, :])
                            ins.then_inc(a_pt, 1)
                        values(2)
                        values(3)
                    pe.wait_ge(a_oc, b * T + T)
                    nc.tensor.matmul(m_psum[:, :], w_proj_a[:, :], ao_a[:, :], start=True, stop=True).then_inc(a_out, 1)
                pe.wait_ge(a_done, B + 1)
                with pe.Fori(0, B // 2) as pair:
                    b0 = pair * 2
                    ln_tensor(pe, b0 + B)

            @block.vector
            def _(dve):
                dve.wait_ge(x_in, 16)
                dve.wait_ge(const_in, 7 * 16)
                dve.wait_ge(const_ready, 6)
                with dve.Fori(0, B // 2) as pair:
                    b0 = pair * 2
                    ln_vector(dve, xn, b0, b0)
                dve.sem_inc(a_done, 1)
                with dve.Fori(0, B) as b:
                    for j in range(T):
                        dve.wait_ge(a_proj, b * T + j + 1)
                        dve.tensor_tensor(qkv_a[:, j, :], m_psum[:, 0:3 * D], bias_a[:, :], ALU.add).then_inc(a_qkv, 1)
                    dve.wait_ge(a_qkv, b * T + T)
                    qk = qkv_a[:, :, 0:2 * D].rearrange("p j (h d) -> p j h d", d=HD)
                    ra = rot_a[:, :, :].rearrange("p j (h d) -> p j h d", d=HD)
                    rb = rot_b[:, :, :].rearrange("p j (h d) -> p j h d", d=HD)
                    half = HD // 2

                    def table(i, lo, hi):
                        return rope_a[:, :, i, lo:hi].unsqueeze(2).broadcast_to([128, T, 2 * HEADS, hi - lo])

                    dve.tensor_tensor(ra, qk, table(0, 0, HD), ALU.mult).then_inc(a_rota, 1)
                    dve.tensor_tensor(rb[:, :, :, 0:half], qk[:, :, :, half:HD], table(1, half, HD), ALU.mult).then_inc(a_rotb, 1)
                    dve.tensor_tensor(rb[:, :, :, half:HD], qk[:, :, :, 0:half], table(1, 0, half), ALU.mult).then_inc(a_rotb, 1)
                    dve.tensor_copy(v_pad[:, :, :].rearrange("p j (h c) -> p j h c", c=128 + HD)[:, :, :, 0:HD],
                                    qkv_a[:, :, 2 * D:3 * D].rearrange("p j (h d) -> p j h d", d=HD)).then_inc(a_vpad, 1)
                    dve.wait_ge(a_rota, b + 1)
                    dve.wait_ge(a_rotb, 2 * b + 2)
                    dve.tensor_tensor(qk_pad[:, :, :, 0:HD], ra, rb, ALU.add).then_inc(a_pad, 1)

                    def maximum(g):
                        n = (g // 4 + 1) * 128
                        dve.wait_ge(a_sc, b * G + g + 1)
                        dve.tensor_reduce(st_a[:, 0, :], sc_psum[:, :, 0:n], AX.X, ALU.max).then_inc(a_max, 1)
                        dve.wait_ge(a_max, b * G + g + 1)
                        dve.tensor_scalar(st_a[:, 1, :], st_a[:, 0, :], -A_SCALE, None, ALU.mult).then_inc(a_nmax, 1)

                    def normalise(g):
                        n = (g // 4 + 1) * 128
                        dve.wait_ge(a_exp, (b * G + g) * 4 + 4)
                        dve.reciprocal(st_a[:, 3, :], st_a[:, 2, :]).then_inc(a_rec, 1)
                        dve.wait_ge(a_rec, b * G + g + 1)
                        dve.tensor_tensor(pn_a[:, :, 0:n], p_a[:, :, 0:n],
                                          st_a[:, 3, :].unsqueeze(2).broadcast_to([128, 4, n]), ALU.mult).then_inc(a_pn, 1)

                    maximum(0)
                    normalise(0)
                    for g in range(G):
                        n = (g // 4 + 1) * 128
                        if g + 1 < G:
                            maximum(g + 1)
                        for h in (1, 3):
                            dve.wait_ge(a_pt, (b * G + g) * 4 + h + 1)
                            dve.tensor_copy(pT_a[:, 1, 0:n], tr_psum[:, 1, 0:n]).then_inc(a_ptc_dve, 1)
                        if g + 1 < G:
                            normalise(g + 1)
                    dve.wait_ge(a_out, b + 1)
                    dve.scalar_tensor_tensor(x1[:, b, :], m_psum[:, :], bias_proj[:, :], x1[:, b, :],
                                             ALU.add, ALU.add).then_inc(a_done, 1)
                with dve.Fori(0, B // 2) as pair:
                    b0 = pair * 2
                    ln_vector(dve, xres, b0, b0 + B)
        part.close()

        part = ExitStack()
        w_qkv = sb(part, "w_qkv", [128, 3 * INNER])
        w_o = sb(part, "w_o", [128, INNER // 128, D])
        w_1 = sb(part, "w_1", [128, 2 * FF])
        w_2 = sb(part, "w_2", [128, 3, D])
        vec = sb(part, "vec", [128, NVEC])
        rope_base = sb(part, "rope_base", [128, T, 4 * WD])
        scale_bc = sb(part, "scale_bc", [128, 4 * WD])
        rope = sb(part, "rope", [128, T, 4, WD])
        xs = sb(part, "xs", [128, WIN + S])
        raw = sb(part, "raw", [128, 2, 2, HALF * WD])
        sq = sb(part, "sq", [128, 2, 2 * HALF, WD])
        ss = sb(part, "ss", [128, 2, 2 * HALF])
        ssm = sb(part, "ssm", [128, 2 * HALF])
        rn = sb(part, "rn", [128, 2, 2 * HALF])
        power = sb(part, "power", [128, 2 * HALF])
        rota = sb(part, "rota", [128, 2, 2, HALF * WD])
        rotb = sb(part, "rotb", [128, 2, 2, HALF * WD])
        rots = sb(part, "rots", [128, 2, 2 * HALF, WD])
        qkn = sb(part, "qkn", [128, 2, 2, HALF * WD])
        v_t = sb(part, "v_t", [128, 4, T, HALF * WD // 2])
        qT = sb(part, "qT", [128, 2, 4, 128])
        kT = sb(part, "kT", [128, 8, WIN + S])
        pr = sb(part, "pr", [128, 2, HALF, WD])
        pe_ = sb(part, "pe_", [128, 2, HALF, WD])
        mx = sb(part, "mx", [128, 2, HALF])
        den = sb(part, "den", [128, 2, HALF])
        rden = sb(part, "rden", [128, 2, HALF])
        pT = sb(part, "pT", [128, 2, HALF * WD])
        o_t = sb(part, "o_t", [128, 2, HALF * WD])
        oT = sb(part, "oT", [128, 2, 4, 128])
        hid = rota[:, :, :, :].rearrange("p k q t -> p (k q) t")
        gel = rotb[:, :, 0, :]
        pj_psum = ps(part, "pj_psum", [128, 2, S])
        t_psum = ps(part, "t_psum", [128, S])
        s_psum = ps(part, "s_psum", [128, 2, S])
        ov_psum = ps(part, "ov_psum", [128, 2, S])
        ow_psum = ps(part, "ow_psum", [128, S])

        attn_w_in = sem("attn_w_in")
        ffn_w_in = sem("ffn_w_in")
        pad_zero = sem("pad_zero")
        base_in = sem("base_in")
        rope_ready = sem("rope_ready")
        attn_done = sem("attn_done")
        ffn_done = sem("ffn_done")
        xs_ready = sem("xs_ready")
        proj_done = sem("proj_done")
        proj_read = sem("proj_read")
        sq_ready = sem("sq_ready")
        ss_ready = sem("ss_ready")
        ssm_ready = sem("ssm_ready")
        rn_ready = sem("rn_ready")
        rotb_ready = sem("rotb_ready")
        rots_ready = sem("rots_ready")
        qkn_ready = sem("qkn_ready")
        t_done = sem("t_done")
        t_read = sem("t_read")
        s_done = sem("s_done")
        mx_ready = sem("mx_ready")
        sub_ready = sem("sub_ready")
        exp_ready = sem("exp_ready")
        den_ready = sem("den_ready")
        rden_ready = sem("rden_ready")
        pt_done = sem("pt_done")
        pt_read = sem("pt_read")
        pv_done = sem("pv_done")
        o_ready = sem("o_ready")
        ot_done = sem("ot_done")
        ot_read = sem("ot_read")
        wo_done = sem("wo_done")
        up_done = sem("up_done")
        gel_ready = sem("gel_ready")
        hid_ready = sem("hid_ready")
        down_done = sem("down_done")
        fin = sem("fin")
        out_done = sem("out_done")

        ATT_IN = 3 * 16
        FFN_IN = 3 * 16
        HW = HALF * WD

        def up_bank(c, gate):
            return (pj_psum, s_psum)[c % 2][:, gate, :]

        ln_bank = [pj_psum[:, 0, :], pj_psum[:, 1, :], s_psum[:, 0, :], s_psum[:, 1, :]]

        with nc.Block() as block:
            @block.sync
            def _(sp):
                sp.dma_start(rope_base[:, :, :], win_rope).then_inc(base_in, 16)
                with sp.Fori(0, LAYERS) as l:
                    sp.wait_ge(attn_done, l * (B * T) + 1)
                    sp.dma_start(w_qkv[:, :], wqkv[l, :, :]).then_inc(attn_w_in, 16)
                    sp.dma_start(w_o[:, :, :], wo[l, :, :, :]).then_inc(attn_w_in, 16)
                    sp.dma_start(scale_bc[:, :], qk_scale[l, :].partition_broadcast(128)).then_inc(attn_w_in, 16)
                    sp.wait_ge(ffn_done, l * B + B)
                    sp.dma_start(vec[:, :], vecs[l, :, :]).then_inc(ffn_w_in, 16)
                    sp.dma_start(w_1[:, :], w1[l, :, :]).then_inc(ffn_w_in, 16)
                    sp.dma_start(w_2[:, :, :], w2[l, :, :, :]).then_inc(ffn_w_in, 16)
                with sp.Fori(0, B) as b:
                    sp.wait_ge(fin, b + 1)
                    sp.dma_start(outT[:, b, :], x1[:, b, :]).then_inc(out_done, 16)
                sp.wait_ge(out_done, 16 * B)

            @block.gpsimd
            def _(pool):
                pool.memset(power[:, :], -0.5).then_inc(pad_zero, 1)
                pool.memset(xs[:, 0:WIN + 1], 0.0).then_inc(pad_zero, 1)
                pool.memset(kT[:, :, 0:WIN], 0.0).then_inc(pad_zero, 1)
                pool.memset(ln_x[:, :, 0:1], 0.0).then_inc(pad_zero, 1)
                pool.wait_ge(pad_zero, 4)
                pool.wait_ge(base_in, 16)
                with pool.Fori(0, LAYERS) as l:
                    pool.wait_ge(attn_w_in, l * ATT_IN + ATT_IN)
                    pool.tensor_tensor(rope[:, :, :, :].rearrange("p j f d -> p j (f d)"), rope_base[:, :, :],
                                       scale_bc[:, :].unsqueeze(1).broadcast_to([128, T, 4 * WD]), ALU.mult).then_inc(rope_ready, 1)
                    with pool.Fori(0, B) as b:
                        base = (l * B + b) * STEPS
                        for i in range(STEPS):
                            n = base + i
                            k = i % 2
                            pool.wait_ge(rotb_ready, 2 * n + 2)
                            pool.tensor_tensor(flat(rots[:, k, :, :]), flat(rota[:, k, :, :]), flat(rotb[:, k, :, :]),
                                               ALU.add).then_inc(rots_ready, 1)
                            pool.wait_ge(ss_ready, n + 1)
                            alone(pool)
                            pool.tensor_scalar(ssm[:, :], ss[:, k, :], 1e-24, None, ALU.max).then_inc(ssm_ready, 1)
                            pool.wait_ge(ssm_ready, n + 1)
                            pool.tensor_tensor(rn[:, k, :], ssm[:, :], power[:, :], ALU.pow).then_inc(rn_ready, 1)

            @block.scalar
            def _(act):
                act.wait_ge(pad_zero, 4)
                act.sem_inc(proj_read, 2)
                act.wait_ge(ln_done, 2 * B)

                def copy_proj(base, i, q):
                    act.wait_ge(proj_done, 4 * (base + i) + q + 1)
                    dst = raw[:, i % 2, q, :] if q < 2 else flat(v_t[:, i % 4, 2 * q - 4:2 * q - 2, :])
                    act.activation(dst, pj_psum[:, q % 2, :], ACT.Copy).then_inc(proj_read, 1)

                def squares(base, i):
                    n = base + i
                    act.wait_ge(proj_read, 4 * n + 4)
                    act.activation(flat(sq[:, i % 2, :, :]), flat(raw[:, i % 2, :, :]), ACT.Square).then_inc(sq_ready, 1)

                def copy_t(base, i, q):
                    j, g = i // 2, i % 2
                    act.wait_ge(t_done, 2 * (base + i) + q + 1)
                    dst = qT[:, i % 2, :, :] if q == 0 else kT[:, 4 * g:4 * g + 4, WIN + 128 * j:WIN + 128 * j + 128]
                    act.activation(dst, t_psum[:, :].rearrange("p (c t) -> p c t", c=4), ACT.Copy).then_inc(t_read, 1)

                def exponentials(base, i):
                    act.wait_ge(sub_ready, base + i + 1)
                    act.activation(flat(pe_[:, i % 2, :, :]), flat(pr[:, i % 2, :, :]), ACT.Exp).then_inc(exp_ready, 1)

                def copy_ot(base, i):
                    act.wait_ge(ot_done, base + i + 1)
                    act.activation(flat(oT[:, i % 2, :, :]), ow_psum[:, :], ACT.Copy).then_inc(ot_read, 1)

                with act.Fori(0, LAYERS) as l:
                    with act.Fori(0, B) as b:
                        u = l * B + b
                        base = u * STEPS
                        act.wait_ge(ffn_done, u + 1)
                        act.activation(xs[0:64, WIN:WIN + S], xres[0:64, b, :], ACT.Copy)
                        act.activation(xs[64:128, WIN + 1:WIN + S], xres[64:128, b, 0:S - 1], ACT.Copy).then_inc(xs_ready, 1)
                        for st in range(STEPS + 3):
                            if st < STEPS:
                                copy_proj(base, st, 0)
                                copy_proj(base, st, 1)
                                copy_proj(base, st, 2)
                                squares(base, st)
                                copy_proj(base, st, 3)
                            if 1 <= st <= STEPS:
                                copy_t(base, st - 1, 0)
                            if 3 <= st:
                                copy_ot(base, st - 3)
                            if 1 <= st <= STEPS:
                                copy_t(base, st - 1, 1)
                            if 1 <= st <= STEPS:
                                exponentials(base, st - 1)
                    act.wait_ge(attn_done, (l + 1) * (B * T) + 1)
                    alone(act)
                    with act.Fori(0, B // 2) as pair:
                        b0 = pair * 2
                        ln_scalar(act, xres, b0, (l + 2) * B + b0, True)
                    with act.Fori(0, B) as b:
                        u = l * B + b
                        for c in range(3):
                            act.wait_ge(up_done, (u * 3 + c) * 2 + 2)
                            if c == 2:
                                act.wait_ge(hid_ready, u * 3 + 1)
                            m = FC[c]
                            act.activation(gel[0:m, c % 2, :], up_bank(c, 1)[0:m, :], ACT.Gelu,
                                           bias=vec[0:m, 6 + c:7 + c]).then_inc(gel_ready, 1)

            @block.tensor
            def _(pe):
                pe.wait_ge(pad_zero, 4)
                pe.wait_ge(ln_done, 2 * B)

                def proj(base, i, q):
                    j, g = i // 2, i % 2
                    col = min(q, 2) * INNER + g * HW
                    pe.wait_ge(proj_read, 4 * (base + i) + q + 1)
                    if q < 2:
                        at = WIN + 128 * j
                        ins = nc.tensor.matmul(pj_psum[:, q, :], xs[:, at:at + 128], w_qkv[:, col:col + HW],
                                               start=True, stop=True)
                    else:
                        for w in (2 * q - 4, 2 * q - 3):
                            at = 128 * j + WIN * w
                            for par in range(2):
                                cols = w_qkv[:, col:col + HW].rearrange("p (c r d) -> p r c d", r=2, d=WD)[:, par, :, :]
                                to = 256 * (w % 2)
                                ins = nc.tensor.matmul(pj_psum[64 * par:64 * par + 64, q % 2, to:to + 256],
                                                       xs[:, at:at + 64], cols, start=True, stop=True)
                    ins.then_inc(proj_done, 1)

                def t_qk(base, i, q):
                    n = base + i
                    if q == 0:
                        pe.wait_ge(qkn_ready, n + 1)
                        if i:
                            pe.wait_ge(pt_read, n)
                    else:
                        pe.wait_ge(t_read, 2 * n + 1)
                    for c in range(4):
                        ins = nc.tensor.transpose(t_psum[:, 128 * c:128 * c + 128],
                                                  qkn[:, i % 2, q, 128 * c:128 * c + 128], ident[:, :])
                    ins.then_inc(t_done, 1)

                def scores(base, i):
                    j, g = i // 2, i % 2
                    pe.wait_ge(t_read, 2 * (base + i) + 2)
                    first = 128 + (0 if j == 0 else 256)
                    for par in range(2):
                        nc.tensor.matmul(s_psum[:, par, 0:256], ident_bf[:, :], mask_bf[:, first:first + 256],
                                         start=True, stop=False)
                    for par in range(2):
                        r = slice(64 * par, 64 * par + 64)
                        for c in range(4):
                            for w in range(4):
                                ins = nc.tensor.matmul(s_psum[32 * w:32 * w + 32, par, 64 * c:64 * c + 64],
                                                       qT[r, i % 2, c, 32 * w:32 * w + 32],
                                                       kT[r, 4 * g + c, 128 * j + 32 * w:128 * j + 32 * w + 64],
                                                       start=False, stop=c == 3)
                    ins.then_inc(s_done, 1)

                def t_p(base, i):
                    pe.wait_ge(exp_ready, base + i + 1)
                    for c in range(4):
                        ins = nc.tensor.transpose(t_psum[:, 128 * c:128 * c + 128],
                                                  flat(pe_[:, i % 2, 2 * c:2 * c + 2, :]), ident[:, :])
                    ins.then_inc(pt_done, 1)

                def values(base, i, par):
                    n = base + i
                    pe.wait_ge(pt_read, n + 1)
                    pe.wait_ge(proj_read, 4 * n + 6)
                    alone(pe)
                    r = slice(64 * par, 64 * par + 64)
                    for c in range(4):
                        for w in range(4):
                            ins = nc.tensor.matmul(ov_psum[32 * w:32 * w + 32, par, 64 * c:64 * c + 64],
                                                   pT[r, i % 2, 128 * c + 32 * w:128 * c + 32 * w + 32],
                                                   v_t[r, i % 4, w, 64 * c:64 * c + 64], start=True, stop=True)
                    if par:
                        ins.then_inc(pv_done, 1)

                def t_o(base, u, i):
                    n = base + i
                    pe.wait_ge(o_ready, n + 1)
                    if i % 2 == 0:
                        pe.wait_ge(attn_done, u * T + i // 2 + 1)
                    else:
                        pe.wait_ge(ot_read, n)
                    for c in range(4):
                        ins = nc.tensor.transpose(ow_psum[:, 128 * c:128 * c + 128],
                                                  o_t[:, i % 2, 128 * c:128 * c + 128], ident[:, :])
                    ins.then_inc(ot_done, 1)

                def out_proj(base, i):
                    pe.wait_ge(ot_read, base + i + 1)
                    for c in range(8):
                        ins = nc.tensor.matmul(ow_psum[:, 0:128], w_o[:, c, :], oT[:, c // 4, c % 4, :],
                                               start=c == 0, stop=c == 7)
                    ins.then_inc(wo_done, 1)

                with pe.Fori(0, LAYERS) as l:
                    pe.wait_ge(attn_w_in, l * ATT_IN + ATT_IN)
                    alone(pe)
                    with pe.Fori(0, B) as b:
                        u = l * B + b
                        base = u * STEPS
                        pe.wait_ge(xs_ready, u + 1)
                        for st in range(STEPS + 3):
                            if st < STEPS:
                                proj(base, st, 0)
                                proj(base, st, 1)
                                proj(base, st, 2)
                            if 2 <= st < STEPS + 2:
                                t_p(base, st - 2)
                            if st < STEPS:
                                proj(base, st, 3)
                            if 1 <= st <= STEPS:
                                t_qk(base, st - 1, 0)
                            if 3 <= st:
                                t_o(base, u, st - 3)
                            if 2 <= st < STEPS + 2:
                                values(base, st - 2, 0)
                            if 1 <= st <= STEPS:
                                t_qk(base, st - 1, 1)
                            if 2 <= st < STEPS + 2:
                                values(base, st - 2, 1)
                            if 1 <= st <= STEPS:
                                scores(base, st - 1)
                            if 3 <= st and (st - 3) % 2:
                                out_proj(base, st - 3)
                    with pe.Fori(0, B // 2) as pair:
                        b0 = pair * 2
                        ln_tensor(pe, (l + 2) * B + b0)
                    pe.wait_ge(ln_done, (l + 3) * B)
                    pe.wait_ge(ffn_w_in, l * FFN_IN + FFN_IN)
                    alone(pe)
                    with pe.Fori(0, B) as b:
                        u = l * B + b
                        for c in range(3):
                            if c == 2:
                                pe.wait_ge(hid_ready, u * 3 + 1)
                            for gate in range(2):
                                at = gate * FF + 128 * c
                                nc.tensor.matmul(up_bank(c, gate)[0:FC[c], :], w_1[:, at:at + FC[c]], xn[:, b, :],
                                                 start=True, stop=True).then_inc(up_done, 1)
                        pe.wait_ge(ffn_done, u + B)
                        for c in range(3):
                            pe.wait_ge(hid_ready, u * 3 + c + 1)
                            ins = nc.tensor.matmul(ow_psum[:, :], w_2[0:FC[c], c, :], hid[0:FC[c], c, :],
                                                   start=c == 0, stop=c == 2)
                        ins.then_inc(down_done, 1)

            @block.vector
            def _(dve):
                dve.wait_ge(pad_zero, 4)
                dve.wait_ge(ln_done, 2 * B)
                dve.sem_inc(attn_done, 1)
                dve.sem_inc(ffn_done, B)

                def heads(ap):
                    return ap.rearrange("p (h d) -> p h d", d=WD)

                def rotate(base, i):
                    k, j, half = i % 2, i // 2, WD // 2
                    dve.wait_ge(proj_read, 4 * (base + i) + 4)
                    x = raw[:, k, :, :].rearrange("p q (h d) -> p q h d", d=WD)
                    y = rotb[:, k, :, :].rearrange("p q (h d) -> p q h d", d=WD)

                    def table(f, lo, hi):
                        t = rope[:, j, :, :].rearrange("p (q f) d -> p q f d", f=2)[:, :, f, lo:hi]
                        return t.unsqueeze(2).broadcast_to([128, 2, HALF, hi - lo])

                    dve.tensor_tensor(rota[:, k, :, :].rearrange("p q (h d) -> p q h d", d=WD), x, table(0, 0, WD), ALU.mult)
                    dve.tensor_tensor(y[:, :, :, 0:half], x[:, :, :, half:WD], table(1, half, WD), ALU.mult).then_inc(rotb_ready, 1)
                    dve.tensor_tensor(y[:, :, :, half:WD], x[:, :, :, 0:half], table(1, 0, half), ALU.mult).then_inc(rotb_ready, 1)

                def sum_squares(base, i):
                    dve.wait_ge(sq_ready, base + i + 1)
                    dve.tensor_reduce(ss[:, i % 2, :], sq[:, i % 2, :, :], AX.X, ALU.add).then_inc(ss_ready, 1)

                def copy_pt(base, i):
                    dve.wait_ge(pt_done, base + i + 1)
                    dve.tensor_copy(pT[:, i % 2, :], t_psum[:, :]).then_inc(pt_read, 1)

                def subtract_max(base, i):
                    n, k = base + i, i % 2
                    s = s_psum[:, :, 0:256].rearrange("p r (c d) -> p r c d", d=WD)
                    dve.wait_ge(s_done, n + 1)
                    dve.tensor_reduce(mx[:, k, :].rearrange("p (r c) -> p r c", r=2), s, AX.X, ALU.max).then_inc(mx_ready, 1)
                    dve.wait_ge(mx_ready, n + 1)
                    dve.tensor_tensor(pr[:, k, :, :].rearrange("p (c r) d -> p r c d", r=2), s,
                                      mx[:, k, :].rearrange("p (r c) -> p r c", r=2).unsqueeze(3).broadcast_to([128, 2, 4, WD]),
                                      ALU.subtract).then_inc(sub_ready, 1)

                def normalise_qk(base, i):
                    n, k = base + i, i % 2
                    dve.wait_ge(rots_ready, n + 1)
                    dve.wait_ge(rn_ready, n + 1)
                    dve.tensor_tensor(flat(qkn[:, k, :, :]).rearrange("p (h d) -> p h d", d=WD), rots[:, k, :, :],
                                      rn[:, k, :].unsqueeze(2).broadcast_to([128, 2 * HALF, WD]), ALU.mult).then_inc(qkn_ready, 1)

                def sums(base, i):
                    n, k = base + i, i % 2
                    dve.wait_ge(exp_ready, n + 1)
                    dve.tensor_reduce(den[:, k, :], pe_[:, k, :, :], AX.X, ALU.add).then_inc(den_ready, 1)
                    dve.wait_ge(den_ready, n + 1)
                    dve.reciprocal(rden[:, k, :], den[:, k, :]).then_inc(rden_ready, 1)

                def outputs(base, i):
                    n, k = base + i, i % 2
                    dve.wait_ge(pv_done, n + 1)
                    dve.wait_ge(rden_ready, n + 1)
                    dve.tensor_tensor(o_t[:, k, :].rearrange("p (c r d) -> p r c d", r=2, d=WD),
                                      ov_psum[:, :, 0:256].rearrange("p r (c d) -> p r c d", d=WD),
                                      rden[:, k, :].rearrange("p (c r) -> p r c", r=2).unsqueeze(3).broadcast_to([128, 2, 4, WD]),
                                      ALU.mult).then_inc(o_ready, 1)

                with dve.Fori(0, LAYERS) as l:
                    dve.wait_ge(rope_ready, l + 1)
                    dve.wait_ge(ffn_done, l * B + B)
                    alone(dve)
                    with dve.Fori(0, B) as b:
                        u = l * B + b
                        base = u * STEPS
                        for st in range(STEPS + 3):
                            if 2 <= st < STEPS + 2:
                                copy_pt(base, st - 2)
                            if st < STEPS:
                                rotate(base, st)
                                sum_squares(base, st)
                            if 2 <= st < STEPS + 2:
                                outputs(base, st - 2)
                            if 1 <= st <= STEPS:
                                subtract_max(base, st - 1)
                            if st < STEPS:
                                normalise_qk(base, st)
                            if 1 <= st <= STEPS:
                                sums(base, st - 1)
                            if 3 <= st and (st - 3) % 2:
                                j = (st - 3) // 2
                                dve.wait_ge(wo_done, u * T + j + 1)
                                x = xres[:, b, 128 * j:128 * j + 128]
                                dve.tensor_tensor(x, x, ow_psum[:, 0:128], ALU.add).then_inc(attn_done, 1)
                    dve.wait_ge(ffn_w_in, l * FFN_IN + FFN_IN)
                    dve.wait_ge(attn_done, (l + 1) * (B * T) + 1)
                    alone(dve)
                    with dve.Fori(0, B // 2) as pair:
                        b0 = pair * 2
                        ln_vector(dve, xn, b0, (l + 2) * B + b0, vec[:, 0:1], vec[:, 1:2])
                    with dve.Fori(0, B) as b:
                        u = l * B + b
                        for c in range(3):
                            m = FC[c]
                            dve.wait_ge(gel_ready, u * 3 + c + 1)
                            dve.scalar_tensor_tensor(hid[0:m, c, :], up_bank(c, 0)[0:m, :], vec[0:m, 3 + c:4 + c],
                                                     gel[0:m, c % 2, :], ALU.add, ALU.mult).then_inc(hid_ready, 1)
                        dve.wait_ge(down_done, u + 1)
                        dve.scalar_tensor_tensor(xres[:, b, :], ow_psum[:, :], vec[:, 2:3], xres[:, b, :],
                                                 ALU.add, ALU.add).then_inc(ffn_done, 1)
                dve.wait_ge(ffn_done, LAYERS * B + B)
                with dve.Fori(0, B) as b:
                    dve.tensor_tensor(x1[:, b, :], x1[:, b, :], xres[:, b, :], ALU.add).then_inc(fin, 1)
        part.close()


def rotation_tables():
    f = np.float32
    half = HD // 2
    freqs = f(1.0) / f(10000.0) ** (np.arange(half, dtype=f) / f(half))
    ang = np.arange(S, dtype=f)[:, None] * freqs[None, :]
    a = np.stack([np.concatenate([np.cos(ang), np.cos(ang)], -1), np.concatenate([np.sin(ang), -np.sin(ang)], -1)], 1)
    a_rope = a.reshape(T, 128, 2, HD).transpose(1, 0, 2, 3)
    hf = np.arange(0, WD, 2, dtype=f)
    inv = f(1.0) / f(10000.0) ** (hf / f(WD))
    t = np.arange(S, dtype=f)
    ang = t[:, None] * inv[None, :]
    base = (hf + f(0.4 * WD)) / f(1.4 * WD)
    scale = base[None, :] ** ((t - f(S // 2)) / f(WIN // 2))[:, None]
    c, s = np.cos(ang), np.sin(ang)
    rows = []
    for k in (scale * f(QK_SCALE), f(1.0) / scale):
        rows += [np.concatenate([c * k, c * k], -1), np.concatenate([s * k, -s * k], -1)]
    win = np.stack(rows, 1).reshape(T, 128, 4 * WD).transpose(1, 0, 2)
    return np.ascontiguousarray(a_rope, f), np.ascontiguousarray(win, f)


def mask_tables():
    q = np.arange(128)
    causal = np.where(q[None, :] > q[:, None], MASKED, 0.0)
    r, k = (q % WIN)[:, None], np.arange(2 * WIN)[None, :]
    ok = np.where(k < WIN, k >= r, k - WIN <= r)
    first = ok & ~((q[:, None] < WIN) & (k < WIN))
    w = [np.tile(np.where(m, 0.0, MASKED), (1, 4)) for m in (first, ok)]
    return np.concatenate([causal] + w, 1).astype(np.float32)


def kernel(**inputs):
    import concourse.bacc as bacc
    from concourse.bass_utils import run_bass_kernel_spmd as run

    a = {k.replace("L0_", ""): np.asarray(v) for k, v in inputs.items()}
    a_rope, win_rope = rotation_tables()
    qs, ks = a["ffn_q_scale"], a["ffn_k_scale"]

    def columns(v):
        return np.pad(v, ((0, 0), (0, 384 - FF))).reshape(LAYERS, 3, 128).transpose(0, 2, 1)

    cols = [a["ffn_ln_g"][:, :, None], a["ffn_ln_b"][:, :, None], a["ffn_b2"][:, :, None],
            columns(a["ffn_b1"][:, :FF]), columns(a["ffn_b1"][:, FF:])]
    arrays = {
        "x_t": a["attn_x"].transpose(2, 0, 1),
        "a_w_t": a["attn_qkv_w"].T, "a_b": a["attn_qkv_b"],
        "a_proj_t": a["attn_proj_w"].T, "a_proj_b": a["attn_proj_b"][:, None],
        "a_rope": a_rope, "win_rope": win_rope, "masks": mask_tables(), "identity": np.eye(128, dtype=np.float32),
        "w_qkv": a["ffn_Wqkv"],
        "w_o": a["ffn_Wo"].reshape(LAYERS, INNER // 128, 128, D).transpose(0, 2, 1, 3),
        "w_1": a["ffn_W1"],
        "w_2": np.pad(a["ffn_W2"], ((0, 0), (0, 384 - FF), (0, 0))).reshape(LAYERS, 3, 128, D).transpose(0, 2, 1, 3),
        "vecs": np.concatenate(cols, 2),
        "qk_scale": np.concatenate([qs, qs, ks, ks], 1),
    }
    nc = bacc.Bacc("TRN2", target_bir_lowering=False, num_devices=1)
    feed, args = {}, []
    for name, v in arrays.items():
        feed[name] = np.ascontiguousarray(v)
        args.append(nc.dram_tensor("in_" + name, feed[name].shape, mybir.dt.from_np(feed[name].dtype), kind="ExternalInput").ap())
    out = nc.dram_tensor("out_t", (D, B, S), F32, kind="ExternalOutput").ap()
    program(nc, *args, out)
    r = run(nc, [{"in_" + k: v for k, v in feed.items()}], core_ids=[0])
    return np.ascontiguousarray(r.results[0]["out_t"].transpose(1, 2, 0))
```

```python
import numpy as np
import concourse.bass as bass
from concourse import mybir
from contextlib import ExitStack

F32 = mybir.dt.float32
BF16 = mybir.dt.bfloat16
ALU = mybir.AluOpType
ACT = mybir.ActivationFunctionType
AX = mybir.AxisListType

D = 128
B = 8
S = 512
T = S // 128
HEADS = 16
LAYERS = 6

HD = D // HEADS
A_SCALE = 1.0 / float(np.sqrt(HD))
ROWS = 64

WD = 64
INNER = HEADS * WD
WIN = 32
HALF = 8
STEPS = 2 * T
QK_SCALE = 8.0
MASKED = -1.0e30

FF = 341
FC = [128, 128, FF - 256]
EPS = 1e-5
NVEC = 9


def flat(ap):
    return ap.rearrange("p a b -> p (a b)")


def program(nc, xT, a_wT, a_b, a_pT, a_pb, a_rope, win_rope, masks, ident_in,
            wqkv, wo, w1, w2, vecs, qk_scale, outT):
    ctx = ExitStack()
    with ctx:
        def sem(name):
            return ctx.enter_context(nc.semaphore(name))

        def sb(stack, name, shape, dt=F32):
            return stack.enter_context(nc.sbuf_tensor(name, shape, dt))

        def ps(stack, name, shape, dt=F32):
            return stack.enter_context(nc.psum_tensor(name, shape, dt))

        x1 = sb(ctx, "x1", [128, B, S])
        xres = sb(ctx, "xres", [128, B + 1, S])
        xn = sb(ctx, "xn", [128, B, S])
        ident = sb(ctx, "ident", [128, 128])
        ident_bf = sb(ctx, "ident_bf", [128, 128], BF16)
        mean_w = sb(ctx, "mean_w", [128, 128])
        eps_col = sb(ctx, "eps_col", [128, 1])
        mask_bf = sb(ctx, "mask_bf", [128, 128 + 2 * 256], BF16)
        ln_x = sb(ctx, "ln_x", [128, 2, S])
        ln_c = sb(ctx, "ln_c", [128, 2, S])
        ln_sq = sb(ctx, "ln_sq", [128, 2, S])
        ln_std = sb(ctx, "ln_std", [128, 2, S])
        ln_r = ln_sq
        ln_n = ln_std

        const_in = sem("const_in")
        waited = sem("waited")
        const_ready = sem("const_ready")
        x_in = sem("x_in")
        ln_x_ready = sem("ln_x_ready")
        ln_mean_ready = sem("ln_mean_ready")
        ln_c_ready = sem("ln_c_ready")
        ln_sq_ready = sem("ln_sq_ready")
        ln_var_ready = sem("ln_var_ready")
        ln_std_ready = sem("ln_std_ready")
        ln_r_ready = sem("ln_r_ready")
        ln_n_ready = sem("ln_n_ready")
        ln_done = sem("ln_done")

        def alone(engine):
            engine.sem_inc(waited, 1)

        def ln_copy(act, src, b0, shift):
            for k in range(2):
                if shift:
                    act.activation(ln_x[0:64, k, :], src[0:64, b0 + k, :], ACT.Copy)
                    act.activation(ln_x[64:128, k, 1:S], src[64:128, b0 + k, 0:S - 1], ACT.Copy).then_inc(ln_x_ready, 1)
                else:
                    act.activation(ln_x[:, k, :], src[:, b0 + k, :], ACT.Copy).then_inc(ln_x_ready, 1)

        def ln_mean(pe, v, bank):
            for k in range(2):
                pe.wait_ge(ln_x_ready, v + k + 1)
                nc.tensor.matmul(bank[k], mean_w[:, :], ln_x[:, k, :], start=True, stop=True).then_inc(ln_mean_ready, 1)

        def ln_center(dve, v, bank):
            for k in range(2):
                dve.wait_ge(ln_mean_ready, v + k + 1)
                dve.tensor_tensor(ln_c[:, k, :], ln_x[:, k, :], bank[k], ALU.subtract).then_inc(ln_c_ready, 1)

        def ln_square(act, v):
            for k in range(2):
                act.wait_ge(ln_c_ready, v + k + 1)
                act.activation(ln_sq[:, k, :], ln_c[:, k, :], ACT.Square).then_inc(ln_sq_ready, 1)

        def ln_variance(pe, v, bank):
            for k in range(2):
                pe.wait_ge(ln_sq_ready, v + k + 1)
                nc.tensor.matmul(bank[k], mean_w[:, :], ln_sq[:, k, :], start=True, stop=True).then_inc(ln_var_ready, 1)

        def ln_root(act, v, bank):
            for k in range(2):
                act.wait_ge(ln_var_ready, v + k + 1)
                act.activation(ln_std[:, k, :], bank[k], ACT.Sqrt, bias=eps_col[:, :]).then_inc(ln_std_ready, 1)

        def ln_reciprocal(dve, v, k):
            dve.wait_ge(ln_std_ready, v + k + 1)
            dve.reciprocal(ln_r[:, k, :], ln_std[:, k, :]).then_inc(ln_r_ready, 1)

        def ln_finish(dve, dst, b0, v, gain=None, bias=None):
            for k in range(2):
                dve.wait_ge(ln_r_ready, v + k + 1)
                if gain is None:
                    dve.tensor_tensor(dst[:, b0 + k, :], ln_c[:, k, :], ln_r[:, k, :], ALU.mult).then_inc(ln_done, 1)
                else:
                    dve.tensor_tensor(ln_n[:, k, :], ln_c[:, k, :], ln_r[:, k, :], ALU.mult).then_inc(ln_n_ready, 1)
            if gain is not None:
                for k in range(2):
                    dve.wait_ge(ln_n_ready, v + k + 1 - 2 * B)
                    dve.tensor_scalar(dst[:, b0 + k, :], ln_n[:, k, :], gain, bias, ALU.mult, ALU.add).then_inc(ln_done, 1)
            dve.wait_ge(ln_done, v + 2)
            alone(dve)

        def ln_scalar(act, src, b0, v, bank, shift=False):
            ln_copy(act, src, b0, shift)
            ln_square(act, v)
            ln_root(act, v, bank)

        def ln_tensor(pe, v, bank):
            ln_mean(pe, v, bank)
            ln_variance(pe, v, bank)

        def ln_vector(dve, dst, b0, v, bank, gain=None, bias=None):
            ln_center(dve, v, bank)
            for k in range(2):
                ln_reciprocal(dve, v, k)
            ln_finish(dve, dst, b0, v, gain, bias)

        part = ExitStack()
        mask_f = sb(part, "mask_f", [128, 128 + 2 * 256])
        w_qkv_a = sb(part, "w_qkv_a", [128, 3 * D])
        bias_a = sb(part, "bias_a", [128, 3 * D])
        w_proj_a = sb(part, "w_proj_a", [128, D])
        bias_proj = sb(part, "bias_proj", [128, 1])
        rope_a = sb(part, "rope_a", [128, T, 2, HD])
        xa = sb(part, "xa", [128, S])
        qkv_a = sb(part, "qkv_a", [128, T, 3 * D])
        rot_a = sb(part, "rot_a", [128, T, 2 * D])
        rot_b = sb(part, "rot_b", [128, T, 2 * D])
        rest = sb(part, "rest", [128, T, 2 * D])
        qk_st = sb(part, "qk_st", [128, 2, T * HEADS, ROWS], BF16)
        qkT = sb(part, "qkT", [128, 2, 2, HEADS // 2, S], BF16)
        v_a = sb(part, "v_a", [128, 2, T, HEADS, 32])
        mx_a = sb(part, "mx_a", [128, 2, T, 8])
        mx_rest = sb(part, "mx_rest", [128, T, 8])
        mx_st = sb(part, "mx_st", [128, T, 2 * 3 * 4], BF16)
        mx_T = sb(part, "mx_T", [24, S], BF16)
        pT_a = [sb(part, f"pT_a{k}", [128, 4, S - 128 * k]) for k in range(T)]
        o_a = sb(part, "o_a", [128, 2, S])
        rs_a = sb(part, "rs_a", [128, T, 4])
        ao_t = sb(part, "ao_t", [128, T, D])
        ao_a = sb(part, "ao_a", [128, S])
        s1_psum = ps(part, "s1_psum", [128, 2, S])
        s2_psum = ps(part, "s2_psum", [128, 2, S])
        o_psum = ps(part, "o_psum", [128, 2, S])
        tr_psum = ps(part, "tr_psum", [128, 2, S], BF16)
        m_psum = ps(part, "m_psum", [128, S])
        ln_bank = [s1_psum[:, k, :] for k in range(2)]

        a_x = sem("a_x")
        a_proj = sem("a_proj")
        a_qkv = sem("a_qkv")
        a_v = sem("a_v")
        a_rota = sem("a_rota")
        a_rotb = sem("a_rotb")
        a_rope_done = sem("a_rope_done")
        part1_ready = sem("part1_ready")
        rest_ready = sem("rest_ready")
        part2_ready = sem("part2_ready")
        parts_ready = sem("parts_ready")
        tr_done = sem("tr_done")
        tr_read = sem("tr_read")
        s1_done = sem("s1_done")
        max_done = sem("max_done")
        mx_step = sem("mx_step")
        mt_in = sem("mt_in")
        s2_done = sem("s2_done")
        p_ready = sem("p_ready")
        pv_a = sem("pv_a")
        o_read = sem("o_read")
        ot_a = sem("ot_a")
        rs_ready = sem("rs_ready")
        ao_ready = sem("ao_ready")
        aot_done = sem("aot_done")
        aot_read = sem("aot_read")
        a_out = sem("a_out")
        a_done = sem("a_done")

        UNITS1 = [(0, [0, 1, 2, 3])] + [(1, [0, 1]), (1, [2, 3])] + [(j, [e]) for j in (2, 3) for e in range(4)]
        UNITS2 = [(k, [e]) for k in (0, 1) for e in range(4)] + [(2, [0, 1]), (2, [2, 3])] + [(3, [0, 1, 2, 3])]
        NQ = len(UNITS1)
        NU = 4 * NQ

        LAST = {3: 0, 7: 1, 9: 2, 10: 3}

        def unit(units, p):
            quad = p // NQ
            return (quad // 2, (quad + (units is UNITS2)) % 2) + units[p % NQ]

        Q_PARTS = (slice(0, 3), slice(4, 6), slice(3, 4))
        K_PARTS = (slice(2, 5), slice(1, 6, 4), slice(0, 1))
        MROW = 6 * HD

        def st_part(i, n):
            return qk_st[:, i, :, 0:MROW].rearrange("p t (r d) -> p t r d", d=HD)[:, :, (Q_PARTS, K_PARTS)[i][n], :]

        def by_head(tile, i):
            return tile[:, :, :].rearrange("p j (h d) -> p j h d", d=HD)[:, :, HEADS * i:HEADS * i + HEADS, :]

        def spread(ap, reps):
            return ap.unsqueeze(3).broadcast_to([128, T, HEADS, reps, HD])

        def places(ap):
            return ap.rearrange("p (j h) r d -> p j h r d", h=HEADS)

        def since(engine, semaphore, value):
            if not (isinstance(value, int) and value < 1):
                engine.wait_ge(semaphore, value)

        def fills_before(t):
            return 0 if isinstance(t, int) and t < -1 else 10 * t + 14

        def slots(engine, slot):
            slot(-2, 0, True, False, False)
            slot(-1, 1, True, True, False)
            with engine.Fori(0, B // 2 - 1) as pair:
                slot(pair * 2, 0, True, True, True)
                slot(pair * 2 + 1, 1, True, True, True)
            slot(B - 2, 0, False, True, True)
            slot(B - 1, 1, False, False, True)

        FILL_AT = (1, 3, 5, 7)
        PROJ_AT = (2, 4, 6, 8)
        MAXIMA_AT = NU // 2 + 7
        PART1_AT = 20

        with nc.Block() as block:
            @block.sync
            def _(sp):
                sp.dma_start(x1[:, :, :], xT).then_inc(x_in, 16)
                sp.dma_start(ident[:, :], ident_in).then_inc(const_in, 16)
                sp.dma_start(mask_f[:, :], masks).then_inc(const_in, 16)
                sp.dma_start(w_qkv_a[:, :], a_wT).then_inc(const_in, 16)
                sp.dma_start(bias_a[:, :], a_b.partition_broadcast(128)).then_inc(const_in, 16)
                sp.dma_start(w_proj_a[:, :], a_pT).then_inc(const_in, 16)
                sp.dma_start(bias_proj[:, :], a_pb).then_inc(const_in, 16)
                sp.dma_start(rope_a[:, :, :, :], a_rope).then_inc(const_in, 16)

                def slot(t, parity, prep, one, two):
                    if one:
                        for g in range(2):
                            sp.wait_ge(tr_read, fills_before(t) + (5, 9 if prep else 6)[g])
                            for par in range(2):
                                r = 64 * par + MROW
                                sp.dma_start(qkT[r:r + 3, 1 - parity, 0, 4 * g:4 * g + 4, :],
                                             mx_T[12 * par:12 * par + 12, :]).then_inc(mt_in, 16)

                slots(sp, slot)

            @block.gpsimd
            def _(pool):
                pool.memset(mean_w[:, :], 1.0 / D).then_inc(const_ready, 1)
                pool.memset(eps_col[:, :], EPS).then_inc(const_ready, 1)
                pool.memset(v_a[:, :, :, :, :], 1.0).then_inc(const_ready, 1)
                pool.memset(qk_st[:, 0, :, :], 0.0).then_inc(const_ready, 1)
                pool.memset(qk_st[:, 1, :, :], -1.0).then_inc(const_ready, 1)
                pool.wait_ge(const_in, 7 * 16)
                pool.tensor_copy(ident_bf[:, :], ident[:, :]).then_inc(const_ready, 1)
                pool.tensor_copy(mask_bf[:, :], mask_f[:, :]).then_inc(const_ready, 1)
                pool.wait_ge(const_ready, 7)

                def slot(t, parity, prep, one, two):
                    if one:
                        pool.wait_ge(ao_ready, 4 * t + 4)
                        alone(pool)
                        pool.tensor_copy(v_a[:, 1 - parity, :, :, 0:HD],
                                         qkv_a[:, :, 2 * D:3 * D].rearrange("p j (h d) -> p j h d", d=HD)).then_inc(a_v, 1)
                    if prep:
                        s = t + 2
                        half = HD // 2
                        qk = qkv_a[:, :, 0:2 * D].rearrange("p j (h d) -> p j h d", d=HD)
                        ra = rot_a[:, :, :].rearrange("p j (h d) -> p j h d", d=HD)
                        rb = rot_b[:, :, :].rearrange("p j (h d) -> p j h d", d=HD)

                        def table(i, lo, hi):
                            return rope_a[:, :, i, lo:hi].unsqueeze(2).broadcast_to([128, T, 2 * HEADS, hi - lo])

                        pool.wait_ge(a_qkv, 4 * s + 4)
                        since(pool, parts_ready, 2 * s)
                        alone(pool)
                        pool.tensor_tensor(ra, qk, table(0, 0, HD), ALU.mult).then_inc(a_rota, 1)
                        pool.tensor_tensor(rb[:, :, :, 0:half], qk[:, :, :, half:HD], table(1, half, HD), ALU.mult).then_inc(a_rotb, 1)
                        pool.tensor_tensor(rb[:, :, :, half:HD], qk[:, :, :, 0:half], table(1, 0, half), ALU.mult).then_inc(a_rotb, 1)
                        pool.wait_ge(a_rota, s + 1)
                        pool.wait_ge(a_rotb, 2 * s + 2)
                        alone(pool)
                        pool.tensor_tensor(rot_a[:, :, :], rot_a[:, :, :], rot_b[:, :, :], ALU.add).then_inc(a_rope_done, 1)
                        pool.wait_ge(part1_ready, 2 * s + 2)
                        pool.wait_ge(a_rope_done, s + 1)
                        alone(pool)
                        for i in range(2):
                            pool.tensor_tensor(by_head(rest, i), by_head(rot_a, i),
                                               places(st_part(i, 0))[:, :, :, 0, :], ALU.subtract).then_inc(rest_ready, 1)
                        pool.wait_ge(rest_ready, 2 * s + 2)
                        alone(pool)
                        for i in range(2):
                            pool.tensor_copy(places(st_part(i, 1))[:, :, :, 0, :], by_head(rest, i)).then_inc(part2_ready, 1)
                            pool.tensor_copy(places(st_part(i, 1))[:, :, :, 1, :], by_head(rest, i)).then_inc(part2_ready, 1)
                        pool.wait_ge(part2_ready, 4 * s + 4)
                        alone(pool)
                        for i in range(2):
                            pool.tensor_tensor(places(st_part(i, 2))[:, :, :, 0, :], by_head(rest, i),
                                               places(st_part(i, 1))[:, :, :, 0, :], ALU.subtract).then_inc(parts_ready, 1)

                slots(pool, slot)

            @block.scalar
            def _(act):
                act.wait_ge(x_in, 16)
                act.wait_ge(const_ready, 7)
                with act.Fori(0, B // 2) as pair:
                    b0 = pair * 2
                    ln_scalar(act, x1, b0, b0, ln_bank)
                act.wait_ge(ln_done, B)

                def slot(t, parity, prep, one, two):
                    fills = fills_before(t)
                    late = 5 * one

                    def read_fill(at, n, buf, g):
                        act.wait_ge(tr_done, fills + at + 1)
                        pr = 4 * g + 2 * (n % 2)
                        act.activation(qkT[:, buf, n // 2, pr:pr + 2, :], tr_psum[:, :, :], ACT.Copy).then_inc(tr_read, 1)

                    def read_maxima(g):
                        act.wait_ge(tr_done, fills + (5, 9 if prep else 6)[g])
                        since(act, mt_in, 32 * (2 * t + 2 + g))
                        act.activation(mx_T[:, :], tr_psum[0:24, 0, :], ACT.Copy).then_inc(tr_read, 1)

                    def read_output(quad):
                        act.wait_ge(pv_a, 16 * t + 4 * quad + 8)
                        act.wait_ge(ot_a, 4 * t + quad + 1)
                        alone(act)
                        act.activation(o_a[:, quad % 2, :], o_psum[:, quad % 2, :], ACT.Copy).then_inc(o_read, 1)

                    if prep:
                        since(act, a_proj, 4 * (t + 2))
                        alone(act)
                        act.activation(xa[:, :], xn[:, t + 2, :], ACT.Copy).then_inc(a_x, 1)
                    for p in range(NU):
                        if two:
                            _, _, k, es = unit(UNITS2, p)
                            n, w, quad = len(es), 128 * (T - k), p // NQ
                            if quad and p % NQ == 2:
                                read_output(quad - 1)
                            act.wait_ge(s2_done, t * NU + p + 1)
                            act.wait_ge(pv_a, 16 * t + 4 * quad + k + 1)
                            alone(act)
                            act.activation(flat(pT_a[k][:, es[0]:es[0] + n, :]), s2_psum[:, p % 2, 0:n * w], ACT.Exp,
                                           scale=A_SCALE).then_inc(p_ready, 1)
                        if one and p - 1 in FILL_AT:
                            n = FILL_AT.index(p - 1)
                            read_fill(n, n, 1 - parity, 1)
                        if one and p == MAXIMA_AT + 1:
                            read_maxima(0)
                        if prep and p == PART1_AT:
                            act.wait_ge(a_rope_done, t + 3)
                            alone(act)
                            for i in range(2):
                                for r in range(3):
                                    ins = act.activation(places(st_part(i, 0))[:, :, :, r, :], by_head(rot_a, i), ACT.Copy)
                                ins.then_inc(part1_ready, 1)
                    if prep:
                        for n in range(3):
                            read_fill(late + n, n, parity, 0)
                    if one:
                        read_maxima(1)
                    if two:
                        read_output(3)
                    if prep:
                        read_fill(late + 3 + one, 3, parity, 0)
                    if two:
                        act.wait_ge(aot_done, t + 1)
                        act.activation(ao_a[:, :], m_psum[:, :], ACT.Copy).then_inc(aot_read, 1)

                slots(act, slot)
                act.wait_ge(a_done, B + 1)
                with act.Fori(0, B // 2) as pair:
                    b0 = pair * 2
                    ln_scalar(act, x1, b0, b0 + B, ln_bank)

            @block.tensor
            def _(pe):
                pe.wait_ge(const_in, 7 * 16)
                pe.wait_ge(const_ready, 7)
                with pe.Fori(0, B // 2) as pair:
                    b0 = pair * 2
                    ln_tensor(pe, b0, ln_bank)
                pe.wait_ge(ln_done, B)

                def slot(t, parity, prep, one, two):
                    fills, late = fills_before(t), 5 * one

                    def rows(par):
                        return slice(ROWS * par, ROWS * par + ROWS)

                    def scores(p):
                        if one:
                            g1, par1, j, es1 = unit(UNITS1, p)
                            w1 = 128 * (j + 1)
                            if p % (2 * NQ) == 0:
                                since(pe, tr_read, fills + 4 * g1)
                            since(pe, max_done, t * NU + (NU + p - 1))
                        if two:
                            g2, par2, k, es2 = unit(UNITS2, p)
                            w2 = 128 * (T - k)
                            if p % (2 * NQ) == 0:
                                pe.wait_ge(mt_in, 32 * (2 * t + g2 + 1))
                            pe.wait_ge(p_ready, t * NU + p + 1)
                        alone(pe)
                        if one:
                            q, k_ = (qkT[rows(par1), 1 - parity, i, :, :] for i in range(2))
                            for i, e in enumerate(es1):
                                nc.tensor.matmul(s1_psum[:, p % 2, w1 * i:w1 * i + w1], q[:, 4 * g1 + e, 128 * j:128 * j + 128],
                                                 k_[:, 4 * g1 + e, 0:w1], start=i == 0, stop=False)
                        if two:
                            q, k_ = (qkT[rows(par2), parity, i, :, :] for i in range(2))
                            for i, e in enumerate(es2):
                                nc.tensor.matmul(s2_psum[:, p % 2, w2 * i:w2 * i + w2], k_[:, 4 * g2 + e, 128 * k:128 * k + 128],
                                                 q[:, 4 * g2 + e, 128 * k:S], start=i == 0, stop=False)
                        if one:
                            for i, e in enumerate(es1):
                                ins = nc.tensor.matmul(s1_psum[:, p % 2, w1 * i + w1 - 128:w1 * i + w1], ident_bf[:, :],
                                                       mask_bf[:, 0:128], start=False, stop=e == es1[-1])
                            ins.then_inc(s1_done, 1)
                        if two:
                            for i, e in enumerate(es2):
                                ins = nc.tensor.matmul(s2_psum[:, p % 2, w2 * i:w2 * i + 128], mask_bf[:, 0:128],
                                                       ident_bf[:, :], start=False, stop=e == es2[-1])
                            ins.then_inc(s2_done, 1)

                    def values(last):
                        quad, k = last // NQ, LAST[last % NQ]
                        g, par = quad // 2, (quad + 1) % 2
                        if quad == 0 and k == 0:
                            pe.wait_ge(a_v, t + 1)
                        if k == 0:
                            pe.wait_ge(o_read, 4 * t + quad + 1)
                        pe.wait_ge(p_ready, t * NU + last + 3)
                        alone(pe)
                        for e in range(4):
                            ins = nc.tensor.matmul(o_psum[32 * e:32 * e + 32, quad % 2, 128 * k:S],
                                                   v_a[:, parity, k, 8 * g + 2 * e + par, :], pT_a[k][:, e, :],
                                                   start=k == 0, stop=k == T - 1)
                        ins.then_inc(pv_a, 1)

                    def output(quad):
                        pe.wait_ge(o_read, 4 * t + quad + 3)
                        if quad == 0 and prep:
                            pe.wait_ge(a_qkv, 4 * (t + 3))
                        elif quad == 0:
                            pe.wait_ge(a_done, t + 1)
                        else:
                            pe.wait_ge(ao_ready, 4 * t + quad + 4)
                        alone(pe)
                        for j in range(T):
                            ins = nc.tensor.transpose(m_psum[:, 128 * j:128 * j + 128], o_a[:, quad % 2, 128 * j:128 * j + 128],
                                                      ident[:, :])
                        ins.then_inc(ot_a, 1)

                    def fill(at, n, g):
                        since(pe, tr_read, fills + at)
                        alone(pe)
                        pr = 4 * g + 2 * (n % 2)
                        for c in range(2):
                            for j in range(T):
                                r = HEADS * j + 2 * (pr + c)
                                ins = nc.tensor.transpose(tr_psum[:, c, 128 * j:128 * j + 128],
                                                          qk_st[:, n // 2, r:r + 2, :], ident_bf[:, :])
                        ins.then_inc(tr_done, 1)

                    def transpose_maxima(g):
                        since(pe, tr_read, fills + (4, 8 if prep else 5)[g])
                        pe.wait_ge(mx_step, 5 * (2 * t + g + 3))
                        alone(pe)
                        for j in range(T):
                            ins = nc.tensor.transpose(tr_psum[0:24, 0, 128 * j:128 * j + 128], mx_st[:, j, :], ident_bf[:, :])
                        ins.then_inc(tr_done, 1)

                    def project(j):
                        if j == 0:
                            pe.wait_ge(a_x, t + 3)
                            since(pe, a_done, t + 1)
                        else:
                            pe.wait_ge(a_qkv, 4 * (t + 2) + j)
                        alone(pe)
                        nc.tensor.matmul(m_psum[:, 0:3 * D], xa[:, 128 * j:128 * j + 128], w_qkv_a[:, :],
                                         start=True, stop=True).then_inc(a_proj, 1)

                    for p in range(NU):
                        if one or two:
                            scores(p)
                        if two and p >= 2 and (p - 2) % NQ in LAST:
                            values(p - 2)
                        if two and p >= NQ and p % NQ == 4:
                            output(p // NQ - 1)
                        if one and p in FILL_AT:
                            fill(FILL_AT.index(p), FILL_AT.index(p), 1)
                        if prep and p in PROJ_AT:
                            project(PROJ_AT.index(p))
                        if one and p == MAXIMA_AT:
                            transpose_maxima(0)
                    if prep:
                        pe.wait_ge(parts_ready, 2 * (t + 3))
                        fill(late + 0, 0, 0)
                    if two:
                        values(NU - 2)
                    if prep:
                        fill(late + 1, 1, 0)
                    if two:
                        values(NU - 1)
                    if prep:
                        fill(late + 2, 2, 0)
                    if one:
                        transpose_maxima(1)
                    if two:
                        output(3)
                    if prep:
                        fill(late + 3 + one, 3, 0)
                    if two:
                        pe.wait_ge(ao_ready, 4 * t + 8)
                        alone(pe)
                        for j in range(T):
                            ins = nc.tensor.transpose(m_psum[:, 128 * j:128 * j + 128], ao_t[:, j, :], ident[:, :])
                        ins.then_inc(aot_done, 1)
                        pe.wait_ge(aot_read, t + 1)
                        alone(pe)
                        nc.tensor.matmul(m_psum[:, :], w_proj_a[:, :], ao_a[:, :], start=True, stop=True).then_inc(a_out, 1)

                slots(pe, slot)
                pe.wait_ge(a_done, B + 1)
                with pe.Fori(0, B // 2) as pair:
                    b0 = pair * 2
                    ln_tensor(pe, b0 + B, ln_bank)

            @block.vector
            def _(dve):
                dve.wait_ge(x_in, 16)
                dve.wait_ge(const_in, 7 * 16)
                dve.wait_ge(const_ready, 7)
                with dve.Fori(0, B // 2) as pair:
                    b0 = pair * 2
                    ln_vector(dve, xn, b0, b0, ln_bank)
                dve.sem_inc(a_done, 1)
                dve.sem_inc(ao_ready, 4)
                dve.sem_inc(o_read, 2)
                dve.sem_inc(ot_a, 2)
                dve.sem_inc(p_ready, 2)
                dve.sem_inc(pv_a, 4)

                def slot(t, parity, prep, one, two):
                    def maximum(p):
                        g, par, j, es = unit(UNITS1, p)
                        n, w = len(es), 128 * (j + 1)
                        dve.wait_ge(s1_done, t * NU + (NU + p + 1))
                        alone(dve)
                        at = 4 * par + es[0]
                        dve.tensor_reduce(mx_a[:, g, j, at:at + n], s1_psum[:, p % 2, 0:n * w].rearrange("p (e w) -> p e w", w=w),
                                          AX.X, ALU.max).then_inc(max_done, 1)

                    def split_maxima(g, step):
                        n = 2 * t + 2 + g
                        m = mx_a[:, g, :, :].rearrange("p j (a e) -> p j a e", e=4)
                        rest4 = mx_rest[:, :, :].rearrange("p j (a e) -> p j a e", e=4)
                        parts = mx_st[:, :, :].rearrange("p j (a c e) -> p j a c e", a=2, c=3)
                        if step == 0:
                            since(dve, tr_done, fills_before(t) + (-1, 5)[g])
                            dve.wait_ge(max_done, (t + 1) * NU + 2 * NQ * (g + 1))
                        else:
                            dve.wait_ge(mx_step, 5 * n + step)
                        alone(dve)
                        if step % 2 == 0:
                            src = m if step == 0 else rest4
                            ins = dve.tensor_copy(parts[:, :, :, step // 2, :], src)
                        else:
                            src = m if step == 1 else rest4
                            ins = dve.tensor_tensor(rest4, src, parts[:, :, :, step // 2, :], ALU.subtract)
                        ins.then_inc(mx_step, 1)

                    def normalise(quad):
                        g, par = quad // 2, (quad + 1) % 2
                        dve.wait_ge(ot_a, 4 * t + quad + 3)
                        dve.wait_ge(ao_ready, 4 * t + quad + 4)
                        alone(dve)
                        o = m_psum[:, :].rearrange("p (j e d) -> p j e d", j=T, e=4)
                        dve.reciprocal(rs_a[:, :, :], o[:, :, :, HD]).then_inc(rs_ready, 1)
                        dve.wait_ge(rs_ready, 4 * t + quad + 1)
                        alone(dve)
                        dst = ao_t[:, :, 64 * g:64 * g + 64].rearrange("p j (e a d) -> p j e a d", a=2, d=HD)[:, :, :, par, :]
                        dve.tensor_tensor(dst, o[:, :, :, 0:HD], rs_a[:, :, :].unsqueeze(3).broadcast_to([128, T, 4, HD]),
                                          ALU.mult).then_inc(ao_ready, 1)

                    since(dve, mx_step, 5 * (2 * t + 2))
                    for p in range(NU):
                        if two and p >= NQ and p % NQ == 5:
                            normalise(p // NQ - 1)
                        if one:
                            maximum(p)
                            if 0 <= p - 2 * NQ < 5:
                                split_maxima(0, p - 2 * NQ)
                        if prep and p - 1 in PROJ_AT:
                            j = PROJ_AT.index(p - 1)
                            if j == 0:
                                since(dve, a_v, t + 2)
                            dve.wait_ge(a_proj, 4 * (t + 2) + j + 1)
                            alone(dve)
                            dve.tensor_tensor(qkv_a[:, j, :], m_psum[:, 0:3 * D], bias_a[:, :], ALU.add).then_inc(a_qkv, 1)
                    if one:
                        for step in range(5):
                            split_maxima(1, step)
                    if two:
                        normalise(3)
                        dve.wait_ge(a_out, t + 1)
                        alone(dve)
                        dve.scalar_tensor_tensor(x1[:, t, :], m_psum[:, :], bias_proj[:, :], x1[:, t, :],
                                                 ALU.add, ALU.add).then_inc(a_done, 1)

                slots(dve, slot)
                with dve.Fori(0, B // 2) as pair:
                    b0 = pair * 2
                    ln_vector(dve, xres, b0, b0 + B, ln_bank)
        part.close()

        part = ExitStack()
        w_qkv = sb(part, "w_qkv", [128, 3 * INNER])
        w_o = sb(part, "w_o", [128, INNER // 128, D])
        w_1 = sb(part, "w_1", [128, 2 * FF])
        w_2 = sb(part, "w_2", [128, 3, D])
        vec = sb(part, "vec", [128, NVEC])
        rope_base = sb(part, "rope_base", [128, T, 4 * WD])
        scale_bc = sb(part, "scale_bc", [128, 4 * WD])
        rope = sb(part, "rope", [128, T, 4, WD])
        xs = sb(part, "xs", [128, WIN + S])
        raw = sb(part, "raw", [128, 2, 2, HALF * WD])
        sq = sb(part, "sq", [128, 2, 2 * HALF, WD])
        ss = sb(part, "ss", [128, 2, 2 * HALF])
        ssm = sb(part, "ssm", [128, 2 * HALF])
        rn = sb(part, "rn", [128, 2, 2 * HALF])
        power = sb(part, "power", [128, 2 * HALF])
        rota = sb(part, "rota", [128, 2, 2, HALF * WD])
        rotb = sb(part, "rotb", [128, 2, 2, HALF * WD])
        rots = sb(part, "rots", [128, 2, 2 * HALF, WD])
        qkn = sb(part, "qkn", [128, 2, 2, HALF * WD])
        v_t = sb(part, "v_t", [128, 4, T, HALF * WD // 2])
        qT = sb(part, "qT", [128, 2, 4, 128])
        kT = sb(part, "kT", [128, 8, WIN + S])
        pr = sb(part, "pr", [128, 2, HALF, WD])
        pe_ = sb(part, "pe_", [128, 2, HALF, WD])
        mx = sb(part, "mx", [128, 2, HALF])
        den = sb(part, "den", [128, 2, HALF])
        rden = sb(part, "rden", [128, 2, HALF])
        pT = sb(part, "pT", [128, 2, HALF * WD])
        o_t = sb(part, "o_t", [128, 2, HALF * WD])
        oT = sb(part, "oT", [128, 2, 4, 128])
        hid = rota[:, :, :, :].rearrange("p k q t -> p (k q) t")
        gel = rotb[:, :, 0, :]
        pj_psum = ps(part, "pj_psum", [128, 2, S])
        t_psum = ps(part, "t_psum", [128, S])
        s_psum = ps(part, "s_psum", [128, 2, S])
        ov_psum = ps(part, "ov_psum", [128, 2, S])
        ow_psum = ps(part, "ow_psum", [128, S])

        attn_w_in = sem("attn_w_in")
        ffn_w_in = sem("ffn_w_in")
        pad_zero = sem("pad_zero")
        base_in = sem("base_in")
        rope_ready = sem("rope_ready")
        attn_done = sem("attn_done")
        ffn_done = sem("ffn_done")
        xs_ready = sem("xs_ready")
        proj_done = sem("proj_done")
        proj_read = sem("proj_read")
        sq_ready = sem("sq_ready")
        ss_ready = sem("ss_ready")
        ssm_ready = sem("ssm_ready")
        rn_ready = sem("rn_ready")
        rotb_ready = sem("rotb_ready")
        rots_ready = sem("rots_ready")
        qkn_ready = sem("qkn_ready")
        t_done = sem("t_done")
        t_read = sem("t_read")
        s_done = sem("s_done")
        mx_ready = sem("mx_ready")
        sub_ready = sem("sub_ready")
        exp_ready = sem("exp_ready")
        den_ready = sem("den_ready")
        rden_ready = sem("rden_ready")
        pt_done = sem("pt_done")
        pt_read = sem("pt_read")
        pv_done = sem("pv_done")
        o_ready = sem("o_ready")
        ot_done = sem("ot_done")
        ot_read = sem("ot_read")
        wo_done = sem("wo_done")
        up_done = sem("up_done")
        gel_ready = sem("gel_ready")
        hid_ready = sem("hid_ready")
        down_done = sem("down_done")
        fin = sem("fin")
        out_done = sem("out_done")

        ATT_IN = 3 * 16
        FFN_IN = 3 * 16
        HW = HALF * WD

        def up_bank(c, gate):
            return (pj_psum, s_psum)[c % 2][:, gate, :]

        ln_bank = [ov_psum[:, k, :] for k in range(2)]

        HEAD, BODY, TAIL = range(3)
        LAG = 3

        def runs(mode, st, lag):
            return st >= lag if mode == HEAD else st < lag if mode == TAIL else True

        def place(b, u, st, lag):
            back = st < lag
            return (b - 1, u - 1, st - lag + STEPS) if back else (b, u, st - lag)

        def stream(engine, l, step):
            for st in range(STEPS):
                step(HEAD, 0, l * B, st)
            with engine.Fori(1, B) as b:
                for st in range(STEPS):
                    step(BODY, b, l * B + b, st)
            for st in range(LAG):
                step(TAIL, B, l * B + B, st)

        with nc.Block() as block:
            @block.sync
            def _(sp):
                sp.dma_start(rope_base[:, :, :], win_rope).then_inc(base_in, 16)
                with sp.Fori(0, LAYERS) as l:
                    sp.wait_ge(attn_done, l * (B * T) + 1)
                    sp.dma_start(w_qkv[:, :], wqkv[l, :, :]).then_inc(attn_w_in, 16)
                    sp.dma_start(w_o[:, :, :], wo[l, :, :, :]).then_inc(attn_w_in, 16)
                    sp.dma_start(scale_bc[:, :], qk_scale[l, :].partition_broadcast(128)).then_inc(attn_w_in, 16)
                    sp.wait_ge(ffn_done, l * B + B)
                    sp.dma_start(vec[:, :], vecs[l, :, :]).then_inc(ffn_w_in, 16)
                    sp.dma_start(w_1[:, :], w1[l, :, :]).then_inc(ffn_w_in, 16)
                    sp.dma_start(w_2[:, :, :], w2[l, :, :, :]).then_inc(ffn_w_in, 16)
                with sp.Fori(0, B) as b:
                    sp.wait_ge(fin, b + 1)
                    sp.dma_start(outT[:, b, :], x1[:, b, :]).then_inc(out_done, 16)
                sp.wait_ge(out_done, 16 * B)

            @block.gpsimd
            def _(pool):
                pool.memset(power[:, :], -0.5).then_inc(pad_zero, 1)
                pool.memset(xs[:, 0:WIN + 1], 0.0).then_inc(pad_zero, 1)
                pool.memset(kT[:, :, 0:WIN], 0.0).then_inc(pad_zero, 1)
                pool.memset(ln_x[:, :, 0:1], 0.0).then_inc(pad_zero, 1)
                pool.memset(xres[:, B, :], 0.0).then_inc(pad_zero, 1)
                pool.wait_ge(pad_zero, 5)
                pool.wait_ge(base_in, 16)
                with pool.Fori(0, LAYERS) as l:
                    pool.wait_ge(attn_w_in, l * ATT_IN + ATT_IN)
                    pool.tensor_tensor(rope[:, :, :, :].rearrange("p j f d -> p j (f d)"), rope_base[:, :, :],
                                       scale_bc[:, :].unsqueeze(1).broadcast_to([128, T, 4 * WD]), ALU.mult).then_inc(rope_ready, 1)
                    with pool.Fori(0, B) as b:
                        base = (l * B + b) * STEPS
                        for i in range(STEPS):
                            n = base + i
                            k = i % 2
                            pool.wait_ge(rotb_ready, 2 * n + 2)
                            pool.tensor_tensor(flat(rots[:, k, :, :]), flat(rota[:, k, :, :]), flat(rotb[:, k, :, :]),
                                               ALU.add).then_inc(rots_ready, 1)
                            pool.wait_ge(ss_ready, n + 1)
                            alone(pool)
                            pool.tensor_scalar(ssm[:, :], ss[:, k, :], 1e-24, None, ALU.max).then_inc(ssm_ready, 1)
                            pool.wait_ge(ssm_ready, n + 1)
                            pool.tensor_tensor(rn[:, k, :], ssm[:, :], power[:, :], ALU.pow).then_inc(rn_ready, 1)

            @block.scalar
            def _(act):
                act.wait_ge(pad_zero, 5)
                act.sem_inc(proj_read, 2)
                act.wait_ge(ln_done, 2 * B)

                def copy_proj(base, i, q):
                    act.wait_ge(proj_done, 4 * (base + i) + q + 1)
                    dst = raw[:, i % 2, q, :] if q < 2 else flat(v_t[:, i % 4, 2 * q - 4:2 * q - 2, :])
                    act.activation(dst, pj_psum[:, q % 2, :], ACT.Copy).then_inc(proj_read, 1)

                def squares(base, i):
                    n = base + i
                    act.wait_ge(proj_read, 4 * n + 4)
                    act.activation(flat(sq[:, i % 2, :, :]), flat(raw[:, i % 2, :, :]), ACT.Square).then_inc(sq_ready, 1)

                def copy_t(base, i, q):
                    j, g = i // 2, i % 2
                    act.wait_ge(t_done, 2 * (base + i) + q + 1)
                    dst = qT[:, i % 2, :, :] if q == 0 else kT[:, 4 * g:4 * g + 4, WIN + 128 * j:WIN + 128 * j + 128]
                    act.activation(dst, t_psum[:, :].rearrange("p (c t) -> p c t", c=4), ACT.Copy).then_inc(t_read, 1)

                def exponentials(base, i):
                    act.wait_ge(sub_ready, base + i + 1)
                    act.activation(flat(pe_[:, i % 2, :, :]), flat(pr[:, i % 2, :, :]), ACT.Exp).then_inc(exp_ready, 1)

                def copy_pt(base, i):
                    act.wait_ge(pt_done, base + i + 1)
                    act.activation(pT[:, i % 2, :], t_psum[:, :], ACT.Copy).then_inc(pt_read, 1)

                def copy_ot(base, i):
                    act.wait_ge(ot_done, base + i + 1)
                    act.activation(flat(oT[:, i % 2, :, :]), ow_psum[:, :], ACT.Copy).then_inc(ot_read, 1)

                def copy_xs(b, j):
                    to = WIN + 128 * j
                    lo = 0 if j else 1
                    act.activation(xs[0:64, to:to + 128], xres[0:64, b, 128 * j:128 * j + 128], ACT.Copy)
                    act.activation(xs[64:128, to + lo:to + 128], xres[64:128, b, 128 * j + lo - 1:128 * j + 127],
                                   ACT.Copy).then_inc(xs_ready, 1)

                def step(mode, b, u, st):
                    def run(stage, lag, *more):
                        if runs(mode, st, lag):
                            _, v, i = place(b, u, st, lag)
                            stage(v * STEPS, i, *more)
                    run(copy_proj, 0, 0)
                    run(exponentials, 2)
                    run(copy_proj, 0, 1)
                    run(copy_proj, 0, 2)
                    run(copy_pt, 2)
                    run(squares, 0)
                    run(copy_proj, 0, 3)
                    run(copy_ot, 3)
                    run(copy_t, 1, 0)
                    run(copy_t, 1, 1)
                    if mode != TAIL and st % 2 == 0:
                        copy_xs(b + st // 4, (2 + st // 2) % T)

                with act.Fori(0, LAYERS) as l:
                    act.wait_ge(ffn_done, l * B + B)
                    alone(act)
                    copy_xs(0, 0)
                    copy_xs(0, 1)
                    stream(act, l, step)
                    act.wait_ge(attn_done, (l + 1) * (B * T) + 1)
                    alone(act)

                    def gates(b):
                        u = l * B + b
                        for c in range(3):
                            act.wait_ge(up_done, (u * 3 + c) * 2 + 2)
                            if c == 2:
                                act.wait_ge(hid_ready, u * 3 + 1)
                            m = FC[c]
                            act.activation(gel[0:m, c % 2, :], up_bank(c, 1)[0:m, :], ACT.Gelu,
                                           bias=vec[0:m, 6 + c:7 + c]).then_inc(gel_ready, 1)

                    v = (l + 2) * B
                    ln_scalar(act, xres, 0, v, ln_bank, shift=True)
                    with act.Fori(0, B // 2 - 1) as pair:
                        b0 = pair * 2
                        ln_copy(act, xres, b0 + 2, True)
                        gates(b0)
                        ln_square(act, v + b0 + 2)
                        ln_root(act, v + b0 + 2, ln_bank)
                        gates(b0 + 1)
                    gates(B - 2)
                    gates(B - 1)

            @block.tensor
            def _(pe):
                pe.wait_ge(pad_zero, 5)
                pe.wait_ge(ln_done, 2 * B)

                def proj(base, i, q):
                    j, g = i // 2, i % 2
                    col = min(q, 2) * INNER + g * HW
                    pe.wait_ge(proj_read, 4 * (base + i) + q + 1)
                    if q < 2:
                        at = WIN + 128 * j
                        ins = nc.tensor.matmul(pj_psum[:, q, :], xs[:, at:at + 128], w_qkv[:, col:col + HW],
                                               start=True, stop=True)
                    else:
                        for w in (2 * q - 4, 2 * q - 3):
                            at = 128 * j + WIN * w
                            for par in range(2):
                                cols = w_qkv[:, col:col + HW].rearrange("p (c r d) -> p r c d", r=2, d=WD)[:, par, :, :]
                                to = 256 * (w % 2)
                                ins = nc.tensor.matmul(pj_psum[64 * par:64 * par + 64, q % 2, to:to + 256],
                                                       xs[:, at:at + 64], cols, start=True, stop=True)
                    ins.then_inc(proj_done, 1)

                def t_qk(base, i, q):
                    n = base + i
                    if q == 0:
                        pe.wait_ge(qkn_ready, n + 1)
                    else:
                        pe.wait_ge(t_read, 2 * n + 1)
                    for c in range(4):
                        ins = nc.tensor.transpose(t_psum[:, 128 * c:128 * c + 128],
                                                  qkn[:, i % 2, q, 128 * c:128 * c + 128], ident[:, :])
                    ins.then_inc(t_done, 1)

                def scores(base, i):
                    j, g = i // 2, i % 2
                    pe.wait_ge(t_read, 2 * (base + i) + 2)
                    first = 128 + (0 if j == 0 else 256)
                    for par in range(2):
                        nc.tensor.matmul(s_psum[:, par, 0:256], ident_bf[:, :], mask_bf[:, first:first + 256],
                                         start=True, stop=False)
                    for par in range(2):
                        r = slice(64 * par, 64 * par + 64)
                        for c in range(4):
                            for w in range(4):
                                ins = nc.tensor.matmul(s_psum[32 * w:32 * w + 32, par, 64 * c:64 * c + 64],
                                                       qT[r, i % 2, c, 32 * w:32 * w + 32],
                                                       kT[r, 4 * g + c, 128 * j + 32 * w:128 * j + 32 * w + 64],
                                                       start=False, stop=c == 3)
                    ins.then_inc(s_done, 1)

                def t_p(base, i):
                    pe.wait_ge(exp_ready, base + i + 1)
                    for c in range(4):
                        ins = nc.tensor.transpose(t_psum[:, 128 * c:128 * c + 128],
                                                  flat(pe_[:, i % 2, 2 * c:2 * c + 2, :]), ident[:, :])
                    ins.then_inc(pt_done, 1)

                def values(base, i, par):
                    n = base + i
                    pe.wait_ge(pt_read, n + 1)
                    pe.wait_ge(proj_read, 4 * n + 6)
                    alone(pe)
                    r = slice(64 * par, 64 * par + 64)
                    for c in range(4):
                        for w in range(4):
                            ins = nc.tensor.matmul(ov_psum[32 * w:32 * w + 32, par, 64 * c:64 * c + 64],
                                                   pT[r, i % 2, 128 * c + 32 * w:128 * c + 32 * w + 32],
                                                   v_t[r, i % 4, w, 64 * c:64 * c + 64], start=True, stop=True)
                    if par:
                        ins.then_inc(pv_done, 1)

                def t_o(base, i, u):
                    n = base + i
                    pe.wait_ge(o_ready, n + 1)
                    if i % 2 == 0:
                        pe.wait_ge(attn_done, u * T + i // 2 + 1)
                    else:
                        pe.wait_ge(ot_read, n)
                    for c in range(4):
                        ins = nc.tensor.transpose(ow_psum[:, 128 * c:128 * c + 128],
                                                  o_t[:, i % 2, 128 * c:128 * c + 128], ident[:, :])
                    ins.then_inc(ot_done, 1)

                def out_proj(base, i):
                    pe.wait_ge(ot_read, base + i + 1)
                    for c in range(8):
                        ins = nc.tensor.matmul(ow_psum[:, 0:128], w_o[:, c, :], oT[:, c // 4, c % 4, :],
                                               start=c == 0, stop=c == 7)
                    ins.then_inc(wo_done, 1)

                with pe.Fori(0, LAYERS) as l:
                    pe.wait_ge(attn_w_in, l * ATT_IN + ATT_IN)
                    alone(pe)

                    def step(mode, b, u, st):
                        def run(stage, lag, *more):
                            if runs(mode, st, lag):
                                _, v, i = place(b, u, st, lag)
                                stage(v * STEPS, i, *more)
                        if mode != TAIL and st % 2 == 0:
                            pe.wait_ge(xs_ready, l * (B * T + 2) + b * T + st // 2 + 1)
                        run(proj, 0, 0)
                        run(proj, 0, 1)
                        run(proj, 0, 2)
                        run(t_p, 2)
                        run(proj, 0, 3)
                        if runs(mode, st, 3):
                            _, v, i = place(b, u, st, 3)
                            t_o(v * STEPS, i, v)
                        run(values, 2, 0)
                        run(t_qk, 1, 0)
                        run(values, 2, 1)
                        run(t_qk, 1, 1)
                        if (st - 3) % 2:
                            run(out_proj, 3)
                        run(scores, 1)

                    stream(pe, l, step)
                    pe.wait_ge(ffn_w_in, l * FFN_IN + FFN_IN)
                    alone(pe)

                    def feed_forward(b):
                        u = l * B + b
                        for c in range(3):
                            if c == 0:
                                pe.wait_ge(ln_done, (l + 2) * B + b + 1)
                            if c == 2:
                                pe.wait_ge(hid_ready, u * 3 + 1)
                            for gate in range(2):
                                at = gate * FF + 128 * c
                                nc.tensor.matmul(up_bank(c, gate)[0:FC[c], :], w_1[:, at:at + FC[c]], xn[:, b, :],
                                                 start=True, stop=True).then_inc(up_done, 1)
                        pe.wait_ge(ffn_done, u + B)
                        for c in range(3):
                            pe.wait_ge(hid_ready, u * 3 + c + 1)
                            ins = nc.tensor.matmul(ow_psum[:, :], w_2[0:FC[c], c, :], hid[0:FC[c], c, :],
                                                   start=c == 0, stop=c == 2)
                        ins.then_inc(down_done, 1)

                    v = (l + 2) * B
                    ln_tensor(pe, v, ln_bank)
                    with pe.Fori(0, B // 2 - 1) as pair:
                        b0 = pair * 2
                        ln_mean(pe, v + b0 + 2, ln_bank)
                        feed_forward(b0)
                        ln_variance(pe, v + b0 + 2, ln_bank)
                        feed_forward(b0 + 1)
                    feed_forward(B - 2)
                    feed_forward(B - 1)

            @block.vector
            def _(dve):
                dve.wait_ge(pad_zero, 5)
                dve.wait_ge(ln_done, 2 * B)
                dve.sem_inc(attn_done, 1)
                dve.sem_inc(ffn_done, B)

                def heads(ap):
                    return ap.rearrange("p (h d) -> p h d", d=WD)

                def rotate(base, i, own):
                    k, j, half = i % 2, i // 2, WD // 2
                    x = raw[:, k, :, :].rearrange("p q (h d) -> p q h d", d=WD)
                    y = rotb[:, k, :, :].rearrange("p q (h d) -> p q h d", d=WD)

                    def table(f, lo, hi):
                        t = rope[:, j, :, :].rearrange("p (q f) d -> p q f d", f=2)[:, :, f, lo:hi]
                        return t.unsqueeze(2).broadcast_to([128, 2, HALF, hi - lo])

                    if own:
                        dve.wait_ge(proj_read, 4 * (base + i) + 4)
                        dve.tensor_tensor(rota[:, k, :, :].rearrange("p q (h d) -> p q h d", d=WD), x, table(0, 0, WD), ALU.mult)
                        return
                    dve.tensor_tensor(y[:, :, :, 0:half], x[:, :, :, half:WD], table(1, half, WD), ALU.mult).then_inc(rotb_ready, 1)
                    dve.tensor_tensor(y[:, :, :, half:WD], x[:, :, :, 0:half], table(1, 0, half), ALU.mult).then_inc(rotb_ready, 1)

                def sum_squares(base, i):
                    dve.wait_ge(sq_ready, base + i + 1)
                    dve.tensor_reduce(ss[:, i % 2, :], sq[:, i % 2, :, :], AX.X, ALU.add).then_inc(ss_ready, 1)

                def subtract_max(base, i):
                    n, k = base + i, i % 2
                    s = s_psum[:, :, 0:256].rearrange("p r (c d) -> p r c d", d=WD)
                    dve.wait_ge(s_done, n + 1)
                    dve.tensor_reduce(mx[:, k, :].rearrange("p (r c) -> p r c", r=2), s, AX.X, ALU.max).then_inc(mx_ready, 1)
                    dve.wait_ge(mx_ready, n + 1)
                    dve.tensor_tensor(pr[:, k, :, :].rearrange("p (c r) d -> p r c d", r=2), s,
                                      mx[:, k, :].rearrange("p (r c) -> p r c", r=2).unsqueeze(3).broadcast_to([128, 2, 4, WD]),
                                      ALU.subtract).then_inc(sub_ready, 1)

                def normalise_qk(base, i):
                    n, k = base + i, i % 2
                    dve.wait_ge(rots_ready, n + 1)
                    dve.wait_ge(rn_ready, n + 1)
                    dve.tensor_tensor(flat(qkn[:, k, :, :]).rearrange("p (h d) -> p h d", d=WD), rots[:, k, :, :],
                                      rn[:, k, :].unsqueeze(2).broadcast_to([128, 2 * HALF, WD]), ALU.mult).then_inc(qkn_ready, 1)

                def sums(base, i):
                    n, k = base + i, i % 2
                    dve.wait_ge(exp_ready, n + 1)
                    dve.tensor_reduce(den[:, k, :], pe_[:, k, :, :], AX.X, ALU.add).then_inc(den_ready, 1)
                    dve.wait_ge(den_ready, n + 1)
                    dve.reciprocal(rden[:, k, :], den[:, k, :]).then_inc(rden_ready, 1)

                def outputs(base, i):
                    n, k = base + i, i % 2
                    dve.wait_ge(pv_done, n + 1)
                    dve.wait_ge(rden_ready, n + 1)
                    dve.tensor_tensor(o_t[:, k, :].rearrange("p (c r d) -> p r c d", r=2, d=WD),
                                      ov_psum[:, :, 0:256].rearrange("p r (c d) -> p r c d", d=WD),
                                      rden[:, k, :].rearrange("p (c r) -> p r c", r=2).unsqueeze(3).broadcast_to([128, 2, 4, WD]),
                                      ALU.mult).then_inc(o_ready, 1)

                with dve.Fori(0, LAYERS) as l:
                    dve.wait_ge(rope_ready, l + 1)
                    dve.wait_ge(ffn_done, l * B + B)
                    alone(dve)

                    def residual(u, b, i):
                        if i % 2:
                            j = i // 2
                            dve.wait_ge(wo_done, u * T + j + 1)
                            x = xres[:, b, 128 * j:128 * j + 128]
                            dve.tensor_tensor(x, x, ow_psum[:, 0:128], ALU.add).then_inc(attn_done, 1)

                    def step(mode, b, u, st):
                        def run(stage, lag, *more):
                            if runs(mode, st, lag):
                                _, v, i = place(b, u, st, lag)
                                stage(v * STEPS, i, *more)
                        run(subtract_max, 2)
                        run(sums, 2)
                        run(rotate, 0, True)
                        run(normalise_qk, 1)
                        run(rotate, 0, False)
                        run(sum_squares, 0)
                        run(outputs, 2)
                        if runs(mode, st, 3):
                            c, v, i = place(b, u, st, 3)
                            residual(v, c, i)

                    stream(dve, l, step)
                    dve.wait_ge(ffn_w_in, l * FFN_IN + FFN_IN)
                    dve.wait_ge(attn_done, (l + 1) * (B * T) + 1)
                    alone(dve)

                    def hidden(b, chunks):
                        u = l * B + b
                        for c in chunks:
                            m = FC[c]
                            dve.wait_ge(gel_ready, u * 3 + c + 1)
                            dve.scalar_tensor_tensor(hid[0:m, c, :], up_bank(c, 0)[0:m, :], vec[0:m, 3 + c:4 + c],
                                                     gel[0:m, c % 2, :], ALU.add, ALU.mult).then_inc(hid_ready, 1)

                    def down_residual(b):
                        dve.wait_ge(down_done, l * B + b + 1)
                        dve.scalar_tensor_tensor(xres[:, b, :], ow_psum[:, :], vec[:, 2:3], xres[:, b, :],
                                                 ALU.add, ALU.add).then_inc(ffn_done, 1)

                    v = (l + 2) * B
                    gain, bias = vec[:, 0:1], vec[:, 1:2]
                    ln_vector(dve, xn, 0, v, ln_bank, gain, bias)
                    with dve.Fori(0, B // 2 - 1) as pair:
                        b0 = pair * 2
                        ln_center(dve, v + b0 + 2, ln_bank)
                        hidden(b0, (0, 1, 2))
                        down_residual(b0)
                        ln_reciprocal(dve, v + b0 + 2, 0)
                        hidden(b0 + 1, (0,))
                        ln_reciprocal(dve, v + b0 + 2, 1)
                        hidden(b0 + 1, (1, 2))
                        ln_finish(dve, xn, b0 + 2, v + b0 + 2, gain, bias)
                        down_residual(b0 + 1)
                    for b in (B - 2, B - 1):
                        hidden(b, (0, 1, 2))
                        down_residual(b)
                dve.wait_ge(ffn_done, LAYERS * B + B)
                with dve.Fori(0, B) as b:
                    dve.tensor_tensor(x1[:, b, :], x1[:, b, :], xres[:, b, :], ALU.add).then_inc(fin, 1)
        part.close()


def rotation_tables():
    f = np.float32
    half = HD // 2
    freqs = f(1.0) / f(10000.0) ** (np.arange(half, dtype=f) / f(half))
    ang = np.arange(S, dtype=f)[:, None] * freqs[None, :]
    a = np.stack([np.concatenate([np.cos(ang), np.cos(ang)], -1), np.concatenate([np.sin(ang), -np.sin(ang)], -1)], 1)
    a_rope = a.reshape(T, 128, 2, HD).transpose(1, 0, 2, 3)
    hf = np.arange(0, WD, 2, dtype=f)
    inv = f(1.0) / f(10000.0) ** (hf / f(WD))
    t = np.arange(S, dtype=f)
    ang = t[:, None] * inv[None, :]
    base = (hf + f(0.4 * WD)) / f(1.4 * WD)
    scale = base[None, :] ** ((t - f(S // 2)) / f(WIN // 2))[:, None]
    c, s = np.cos(ang), np.sin(ang)
    rows = []
    for k in (scale * f(QK_SCALE), f(1.0) / scale):
        rows += [np.concatenate([c * k, c * k], -1), np.concatenate([s * k, -s * k], -1)]
    win = np.stack(rows, 1).reshape(T, 128, 4 * WD).transpose(1, 0, 2)
    return np.ascontiguousarray(a_rope, f), np.ascontiguousarray(win, f)


def mask_tables():
    q = np.arange(128)
    causal = np.where(q[None, :] > q[:, None], MASKED, 0.0)
    r, k = (q % WIN)[:, None], np.arange(2 * WIN)[None, :]
    ok = np.where(k < WIN, k >= r, k - WIN <= r)
    first = ok & ~((q[:, None] < WIN) & (k < WIN))
    w = [np.tile(np.where(m, 0.0, MASKED), (1, 4)) for m in (first, ok)]
    return np.concatenate([causal] + w, 1).astype(np.float32)


def kernel(**inputs):
    import concourse.bacc as bacc
    from concourse.bass_utils import run_bass_kernel_spmd as run

    a = {k.replace("L0_", ""): np.asarray(v) for k, v in inputs.items()}
    a_rope, win_rope = rotation_tables()
    qs, ks = a["ffn_q_scale"], a["ffn_k_scale"]

    def columns(v):
        return np.pad(v, ((0, 0), (0, 384 - FF))).reshape(LAYERS, 3, 128).transpose(0, 2, 1)

    cols = [a["ffn_ln_g"][:, :, None], a["ffn_ln_b"][:, :, None], a["ffn_b2"][:, :, None],
            columns(a["ffn_b1"][:, :FF]), columns(a["ffn_b1"][:, FF:])]
    arrays = {
        "x_t": a["attn_x"].transpose(2, 0, 1),
        "a_w_t": a["attn_qkv_w"].T, "a_b": a["attn_qkv_b"],
        "a_proj_t": a["attn_proj_w"].T, "a_proj_b": a["attn_proj_b"][:, None],
        "a_rope": a_rope, "win_rope": win_rope, "masks": mask_tables(), "identity": np.eye(128, dtype=np.float32),
        "w_qkv": a["ffn_Wqkv"],
        "w_o": a["ffn_Wo"].reshape(LAYERS, INNER // 128, 128, D).transpose(0, 2, 1, 3),
        "w_1": a["ffn_W1"],
        "w_2": np.pad(a["ffn_W2"], ((0, 0), (0, 384 - FF), (0, 0))).reshape(LAYERS, 3, 128, D).transpose(0, 2, 1, 3),
        "vecs": np.concatenate(cols, 2),
        "qk_scale": np.concatenate([qs, qs, ks, ks], 1),
    }
    nc = bacc.Bacc("TRN2", target_bir_lowering=False, num_devices=1)
    feed, args = {}, []
    for name, v in arrays.items():
        feed[name] = np.ascontiguousarray(v)
        args.append(nc.dram_tensor("in_" + name, feed[name].shape, mybir.dt.from_np(feed[name].dtype), kind="ExternalInput").ap())
    out = nc.dram_tensor("out_t", (D, B, S), F32, kind="ExternalOutput").ap()
    program(nc, *args, out)
    r = run(nc, [{"in_" + k: v for k, v in feed.items()}], core_ids=[0])
    return np.ascontiguousarray(r.results[0]["out_t"].transpose(1, 2, 0))
```

```python
import numpy as np
import concourse.bass as bass
from concourse import mybir
from contextlib import ExitStack

F32 = mybir.dt.float32
BF16 = mybir.dt.bfloat16
F32R = mybir.dt.float32r
ALU = mybir.AluOpType
ACT = mybir.ActivationFunctionType
AX = mybir.AxisListType

D = 128
B = 8
S = 512
T = S // 128
HEADS = 16
LAYERS = 6

HD = D // HEADS
A_SCALE = 1.0 / float(np.sqrt(HD))
ROWS = 64

WD = 64
INNER = HEADS * WD
WIN = 32
HALF = 8
STEPS = 2 * T
QK_SCALE = 8.0
MASKED = -1.0e30

FF = 341
FC = [128, 128, FF - 256]
EPS = 1e-5
NVEC = 9


def flat(ap):
    return ap.rearrange("p a b -> p (a b)")


def program(nc, xT, a_wT, a_b, a_pT, a_pb, a_rope, win_rope, masks, ident_in,
            wqkv, wo, w1, w2, vecs, qk_scale, outT):
    ctx = ExitStack()
    with ctx:
        def sem(name):
            return ctx.enter_context(nc.semaphore(name))

        def sb(stack, name, shape, dt=F32):
            return stack.enter_context(nc.sbuf_tensor(name, shape, dt))

        def ps(stack, name, shape, dt=F32):
            return stack.enter_context(nc.psum_tensor(name, shape, dt))

        x1 = sb(ctx, "x1", [128, B, S])
        xres = sb(ctx, "xres", [128, B + 1, S])
        xn = sb(ctx, "xn", [128, B, S])
        ident = sb(ctx, "ident", [128, 128])
        ident_bf = sb(ctx, "ident_bf", [128, 128], BF16)
        mean_w = sb(ctx, "mean_w", [128, 128])
        eps_col = sb(ctx, "eps_col", [128, 1])
        mask_bf = sb(ctx, "mask_bf", [128, 128 + 2 * 256], BF16)
        ln_x = sb(ctx, "ln_x", [128, 2, S])
        ln_c = sb(ctx, "ln_c", [128, 2, S])
        ln_sq = sb(ctx, "ln_sq", [128, 2, S])
        ln_std = sb(ctx, "ln_std", [128, 2, S])
        ln_r = ln_sq
        ln_n = ln_std

        const_in = sem("const_in")
        waited = sem("waited")
        const_ready = sem("const_ready")
        x_in = sem("x_in")
        ln_x_ready = sem("ln_x_ready")
        ln_mean_ready = sem("ln_mean_ready")
        ln_c_ready = sem("ln_c_ready")
        ln_sq_ready = sem("ln_sq_ready")
        ln_var_ready = sem("ln_var_ready")
        ln_std_ready = sem("ln_std_ready")
        ln_r_ready = sem("ln_r_ready")
        ln_n_ready = sem("ln_n_ready")
        ln_done = sem("ln_done")

        def alone(engine):
            engine.sem_inc(waited, 1)

        def ln_copy(act, src, b0, shift):
            for k in range(2):
                if shift:
                    act.activation(ln_x[0:64, k, :], src[0:64, b0 + k, :], ACT.Copy)
                    act.activation(ln_x[64:128, k, 1:S], src[64:128, b0 + k, 0:S - 1], ACT.Copy).then_inc(ln_x_ready, 1)
                else:
                    act.activation(ln_x[:, k, :], src[:, b0 + k, :], ACT.Copy).then_inc(ln_x_ready, 1)

        def ln_mean(pe, v, bank):
            for k in range(2):
                pe.wait_ge(ln_x_ready, v + k + 1)
                nc.tensor.matmul(bank[k], mean_w[:, :], ln_x[:, k, :], start=True, stop=True).then_inc(ln_mean_ready, 1)

        def ln_center(dve, v, bank):
            for k in range(2):
                dve.wait_ge(ln_mean_ready, v + k + 1)
                dve.tensor_tensor(ln_c[:, k, :], ln_x[:, k, :], bank[k], ALU.subtract).then_inc(ln_c_ready, 1)

        def ln_square(act, v):
            for k in range(2):
                act.wait_ge(ln_c_ready, v + k + 1)
                act.activation(ln_sq[:, k, :], ln_c[:, k, :], ACT.Square).then_inc(ln_sq_ready, 1)

        def ln_variance(pe, v, bank):
            for k in range(2):
                pe.wait_ge(ln_sq_ready, v + k + 1)
                nc.tensor.matmul(bank[k], mean_w[:, :], ln_sq[:, k, :], start=True, stop=True).then_inc(ln_var_ready, 1)

        def ln_root(act, v, bank):
            for k in range(2):
                act.wait_ge(ln_var_ready, v + k + 1)
                act.activation(ln_std[:, k, :], bank[k], ACT.Sqrt, bias=eps_col[:, :]).then_inc(ln_std_ready, 1)

        def ln_reciprocal(dve, v, k):
            dve.wait_ge(ln_std_ready, v + k + 1)
            dve.reciprocal(ln_r[:, k, :], ln_std[:, k, :]).then_inc(ln_r_ready, 1)

        def ln_finish(dve, dst, b0, v, gain=None, bias=None):
            for k in range(2):
                dve.wait_ge(ln_r_ready, v + k + 1)
                if gain is None:
                    dve.tensor_tensor(dst[:, b0 + k, :], ln_c[:, k, :], ln_r[:, k, :], ALU.mult).then_inc(ln_done, 1)
                else:
                    dve.tensor_tensor(ln_n[:, k, :], ln_c[:, k, :], ln_r[:, k, :], ALU.mult).then_inc(ln_n_ready, 1)
            if gain is not None:
                for k in range(2):
                    dve.wait_ge(ln_n_ready, v + k + 1 - 2 * B)
                    dve.tensor_scalar(dst[:, b0 + k, :], ln_n[:, k, :], gain, bias, ALU.mult, ALU.add).then_inc(ln_done, 1)
            dve.wait_ge(ln_done, v + 2)
            alone(dve)

        def ln_scalar(act, src, b0, v, bank, shift=False):
            ln_copy(act, src, b0, shift)
            ln_square(act, v)
            ln_root(act, v, bank)

        def ln_tensor(pe, v, bank):
            ln_mean(pe, v, bank)
            ln_variance(pe, v, bank)

        def ln_vector(dve, dst, b0, v, bank, gain=None, bias=None):
            ln_center(dve, v, bank)
            for k in range(2):
                ln_reciprocal(dve, v, k)
            ln_finish(dve, dst, b0, v, gain, bias)

        part = ExitStack()
        mask_f = sb(part, "mask_f", [128, 128 + 2 * 256])
        w_qkv_a = sb(part, "w_qkv_a", [128, 3 * D])
        bias_a = sb(part, "bias_a", [128, 3 * D])
        w_proj_a = sb(part, "w_proj_a", [128, D])
        bias_proj = sb(part, "bias_proj", [128, 1])
        rope_a = sb(part, "rope_a", [128, T, 2, HD])
        xa = sb(part, "xa", [128, S])
        qkv_a = sb(part, "qkv_a", [128, T, 3 * D])
        rot_a = sb(part, "rot_a", [128, T, 2 * D])
        rot_b = sb(part, "rot_b", [128, T, 2 * D])
        rest = sb(part, "rest", [128, T, 2 * D])
        qk_st = sb(part, "qk_st", [128, 2, T * HEADS, ROWS], BF16)
        qkT = sb(part, "qkT", [128, 2, 2, HEADS // 2, S], BF16)
        v_a = sb(part, "v_a", [128, 2, T, HEADS, 32])
        mx_a = sb(part, "mx_a", [128, 2, T, 8])
        mx_rest = sb(part, "mx_rest", [128, T, 8])
        mx_st = sb(part, "mx_st", [128, T, 2 * 3 * 4], BF16)
        mx_T = sb(part, "mx_T", [24, S], BF16)
        pT_a = [sb(part, f"pT_a{k}", [128, 4, S - 128 * k]) for k in range(T)]
        o_a = sb(part, "o_a", [128, 2, S])
        rs_a = sb(part, "rs_a", [128, T, 4])
        ao_t = sb(part, "ao_t", [128, T, D])
        ao_a = sb(part, "ao_a", [128, S])
        s1_psum = ps(part, "s1_psum", [128, 2, S])
        s2_psum = ps(part, "s2_psum", [128, 2, S])
        o_psum = ps(part, "o_psum", [128, 2, S])
        tr_psum = ps(part, "tr_psum", [128, 2, S], BF16)
        m_psum = ps(part, "m_psum", [128, S])
        ln_bank = [s1_psum[:, k, :] for k in range(2)]

        a_x = sem("a_x")
        a_proj = sem("a_proj")
        a_qkv = sem("a_qkv")
        a_v = sem("a_v")
        a_rota = sem("a_rota")
        a_rotb = sem("a_rotb")
        a_rope_done = sem("a_rope_done")
        part1_ready = sem("part1_ready")
        rest_ready = sem("rest_ready")
        part2_ready = sem("part2_ready")
        part2_again = sem("part2_again")
        parts_ready = sem("parts_ready")
        tr_done = sem("tr_done")
        tr_read = sem("tr_read")
        s1_done = sem("s1_done")
        max_done = sem("max_done")
        mx_step = sem("mx_step")
        mt_in = sem("mt_in")
        s2_done = sem("s2_done")
        p_ready = sem("p_ready")
        pv_a = sem("pv_a")
        o_read = sem("o_read")
        ot_a = sem("ot_a")
        rs_ready = sem("rs_ready")
        ao_ready = sem("ao_ready")
        aot_done = sem("aot_done")
        aot_read = sem("aot_read")
        a_out = sem("a_out")
        a_done = sem("a_done")

        UNITS1 = [(0, [0, 1, 2, 3])] + [(1, [0, 1]), (1, [2, 3])] + [(j, [e]) for j in (2, 3) for e in range(4)]
        UNITS2 = [(k, [e]) for k in (0, 1) for e in range(4)] + [(2, [0, 1]), (2, [2, 3])] + [(3, [0, 1, 2, 3])]
        NQ = len(UNITS1)
        NU = 4 * NQ

        LAST = {3: 0, 7: 1, 9: 2, 10: 3}

        def unit(units, p):
            quad = p // NQ
            return (quad // 2, (quad + (units is UNITS2)) % 2) + units[p % NQ]

        Q_PARTS = (slice(0, 3), slice(4, 6), slice(3, 4))
        K_PARTS = (slice(2, 5), slice(1, 6, 4), slice(0, 1))
        MROW = 6 * HD

        def st_part(i, n):
            return qk_st[:, i, :, 0:MROW].rearrange("p t (r d) -> p t r d", d=HD)[:, :, (Q_PARTS, K_PARTS)[i][n], :]

        def by_head(tile, i):
            return tile[:, :, :].rearrange("p j (h d) -> p j h d", d=HD)[:, :, HEADS * i:HEADS * i + HEADS, :]

        def places(ap):
            return ap.rearrange("p (j h) r d -> p j h r d", h=HEADS)

        def since(engine, semaphore, value):
            if not (isinstance(value, int) and value < 1):
                engine.wait_ge(semaphore, value)

        def fills_before(t):
            if isinstance(t, int) and t < 0:
                return (0, 4)[t + 2]
            if isinstance(t, int) and t == B - 1:
                return 10 * t + 9
            return 10 * t + 13

        def slots(engine, slot):
            slot(-2, 0, (True, False, False), (True, False))
            slot(-1, 1, (True, True, False), (True, True))
            with engine.Fori(0, B // 2 - 1) as pair:
                slot(pair * 2, 0, (True, True, True), (True, True))
                slot(pair * 2 + 1, 1, (True, True, True), (True, True))
            slot(B - 2, 0, (False, True, True), (False, True))
            slot(B - 1, 1, (False, False, True), (False, False))

        HEAD_UNITS = 13
        PROJ_AT = (13, 14, 16, 17)
        LAST_MAXIMA_AT = 13
        FILL_AT = (14, 16, 18, 19)
        MAXIMA_AT = NU // 2 + 7
        PART1_AT = 24
        PART2_AT = 31
        LAST_FILL_AT = (36, 38, 40, 42)
        OUT_AT = 7
        OUT_T_AT, PROJ_OUT_AT = NU + 9, NU + 11

        with nc.Block() as block:
            @block.sync
            def _(sp):
                sp.dma_start(x1[:, :, :], xT).then_inc(x_in, 16)
                sp.dma_start(ident[:, :], ident_in).then_inc(const_in, 16)
                sp.dma_start(mask_f[:, :], masks).then_inc(const_in, 16)
                sp.dma_start(w_qkv_a[:, :], a_wT).then_inc(const_in, 16)
                sp.dma_start(bias_a[:, :], a_b.partition_broadcast(128)).then_inc(const_in, 16)
                sp.dma_start(w_proj_a[:, :], a_pT).then_inc(const_in, 16)
                sp.dma_start(bias_proj[:, :], a_pb).then_inc(const_in, 16)
                sp.dma_start(rope_a[:, :, :, :], a_rope).then_inc(const_in, 16)

                def slot(t, parity, now, after):
                    _, one, two = now

                    def place_maxima(at, buf, g):
                        sp.wait_ge(tr_read, fills_before(t) + at + 1)
                        for par in range(2):
                            r = ROWS * par + MROW
                            sp.dma_start(qkT[r:r + 3, buf, 0, 4 * g:4 * g + 4, :],
                                         mx_T[12 * par:12 * par + 12, :]).then_inc(mt_in, 16)

                    if two:
                        place_maxima(0, parity, 1)
                    if one:
                        place_maxima(two + 4, 1 - parity, 0)

                slots(sp, slot)

            @block.gpsimd
            def _(pool):
                pool.memset(mean_w[:, :], 1.0 / D).then_inc(const_ready, 1)
                pool.memset(eps_col[:, :], EPS).then_inc(const_ready, 1)
                pool.memset(v_a[:, :, :, :, :], 1.0).then_inc(const_ready, 1)
                pool.memset(qk_st[:, 0, :, :], 0.0).then_inc(const_ready, 1)
                pool.memset(qk_st[:, 1, :, :], -1.0).then_inc(const_ready, 1)
                pool.wait_ge(const_in, 7 * 16)
                pool.tensor_copy(ident_bf[:, :], ident[:, :]).then_inc(const_ready, 1)
                pool.tensor_copy(mask_bf[:, :], mask_f[:, :]).then_inc(const_ready, 1)
                pool.wait_ge(const_ready, 7)

                def slot(t, parity, now, after):
                    prep, one, two = now
                    if one:
                        pool.wait_ge(ao_ready, 4 * t + 4)
                        alone(pool)
                        pool.tensor_copy(v_a[:, 1 - parity, :, :, 0:HD],
                                         qkv_a[:, :, 2 * D:3 * D].rearrange("p j (h d) -> p j h d", d=HD)).then_inc(a_v, 1)
                    if prep:
                        s = t + 2
                        half = HD // 2
                        qk = qkv_a[:, :, 0:2 * D].rearrange("p j (h d) -> p j h d", d=HD)
                        ra = rot_a[:, :, :].rearrange("p j (h d) -> p j h d", d=HD)
                        rb = rot_b[:, :, :].rearrange("p j (h d) -> p j h d", d=HD)

                        def table(i, lo, hi):
                            return rope_a[:, :, i, lo:hi].unsqueeze(2).broadcast_to([128, T, 2 * HEADS, hi - lo])

                        pool.wait_ge(a_qkv, 4 * s + 4)
                        since(pool, parts_ready, 2 * s)
                        alone(pool)
                        pool.tensor_tensor(ra, qk, table(0, 0, HD), ALU.mult).then_inc(a_rota, 1)
                        pool.tensor_tensor(rb[:, :, :, 0:half], qk[:, :, :, half:HD], table(1, half, HD), ALU.mult).then_inc(a_rotb, 1)
                        pool.tensor_tensor(rb[:, :, :, half:HD], qk[:, :, :, 0:half], table(1, 0, half), ALU.mult).then_inc(a_rotb, 1)
                        pool.wait_ge(a_rota, s + 1)
                        pool.wait_ge(a_rotb, 2 * s + 2)
                        alone(pool)
                        pool.tensor_tensor(rot_a[:, :, :], rot_a[:, :, :], rot_b[:, :, :], ALU.add).then_inc(a_rope_done, 1)
                        pool.wait_ge(part1_ready, 6 * s + 2)
                        pool.wait_ge(a_rope_done, s + 1)
                        alone(pool)
                        for i in range(2):
                            pool.tensor_tensor(by_head(rest, i), by_head(rot_a, i),
                                               places(st_part(i, 0))[:, :, :, 0, :], ALU.subtract).then_inc(rest_ready, 1)
                        pool.wait_ge(rest_ready, 2 * s + 2)
                        alone(pool)
                        for i in range(2):
                            pool.tensor_copy(places(st_part(i, 1))[:, :, :, 0, :], by_head(rest, i)).then_inc(part2_ready, 1)
                        pool.wait_ge(part2_ready, 2 * s + 2)
                        alone(pool)
                        for i in range(2):
                            pool.tensor_tensor(places(st_part(i, 2))[:, :, :, 0, :], by_head(rest, i),
                                               places(st_part(i, 1))[:, :, :, 0, :], ALU.subtract).then_inc(parts_ready, 1)

                slots(pool, slot)

            @block.scalar
            def _(act):
                act.wait_ge(x_in, 16)
                act.wait_ge(const_ready, 7)
                with act.Fori(0, B // 2) as pair:
                    b0 = pair * 2
                    ln_scalar(act, x1, b0, b0, ln_bank)
                act.wait_ge(ln_done, B)

                def slot(t, parity, now, after):
                    prep, one, two = now
                    fills = fills_before(t)

                    def read_fill(at, n, buf, g):
                        act.wait_ge(tr_done, fills + at + 1)
                        pr = 4 * g + 2 * (n % 2)
                        act.activation(qkT[:, buf, n // 2, pr:pr + 2, :], tr_psum[:, :, :], ACT.Copy).then_inc(tr_read, 1)

                    def read_maxima(at, before):
                        act.wait_ge(tr_done, fills + at + 1)
                        since(act, mt_in, 32 * before)
                        act.activation(mx_T[:, :], tr_psum[0:24, 0, :], ACT.Copy).then_inc(tr_read, 1)

                    def read_output(u, quad):
                        act.wait_ge(pv_a, 16 * t + 16 * u + 4 * quad + 8)
                        act.wait_ge(ot_a, 4 * t + 4 * u + quad + 1)
                        alone(act)
                        act.activation(o_a[:, quad % 2, :], o_psum[:, quad % 2, :], ACT.Copy).then_inc(o_read, 1)

                    def exponentials(u, p):
                        _, _, k, es = unit(UNITS2, p)
                        n, w, quad = len(es), 128 * (T - k), p // NQ
                        act.wait_ge(s2_done, t * NU + (u * NU + p + 1))
                        act.wait_ge(pv_a, 16 * t + (16 * u + 4 * quad + k + 1))
                        alone(act)
                        act.activation(flat(pT_a[k][:, es[0]:es[0] + n, :]), s2_psum[:, p % 2, 0:n * w], ACT.Exp,
                                       scale=A_SCALE).then_inc(p_ready, 1)

                    def first_parts(i, r):
                        if i == 0 and r == 0:
                            act.wait_ge(a_rope_done, t + 3)
                            alone(act)
                        act.activation(places(st_part(i, 0))[:, :, :, r, :], by_head(rot_a, i), ACT.Copy).then_inc(part1_ready, 1)

                    if prep:
                        since(act, a_proj, 4 * (t + 2))
                        alone(act)
                        act.activation(xa[:, :], xn[:, t + 2, :], ACT.Copy).then_inc(a_x, 1)
                    for P in range(HEAD_UNITS, NU + HEAD_UNITS):
                        u, p = P // NU, P % NU
                        if two and P == LAST_MAXIMA_AT:
                            read_maxima(0, 2 * t + 1)
                        if one and P - 1 in FILL_AT:
                            n = FILL_AT.index(P - 1)
                            read_fill(two + n, n, 1 - parity, 1)
                        if one and P == MAXIMA_AT + 1:
                            read_maxima(two + 4, 2 * t + 2)
                        if prep and P - 1 in LAST_FILL_AT:
                            n = LAST_FILL_AT.index(P - 1)
                            read_fill(two + 5 * one + n, n, parity, 0)
                        if (two, after[1])[u]:
                            exponentials(u, p)
                        if P % NQ == 1 and (two, after[1])[P // NQ // 5]:
                            read_output(P // NQ // 5, (P // NQ - 1) % 4)
                        if prep and PART1_AT <= P < PART1_AT + 4:
                            r = P - PART1_AT - 1
                            if P == PART1_AT:
                                first_parts(0, 0)
                                first_parts(1, 0)
                            elif r < 2:
                                first_parts(r, 1)
                            else:
                                first_parts(0, 2)
                                first_parts(1, 2)
                        if two and P == OUT_T_AT + 1:
                            act.wait_ge(aot_done, t + 1)
                            alone(act)
                            act.activation(ao_a[:, :], m_psum[:, :], ACT.Copy).then_inc(aot_read, 1)

                slots(act, slot)
                act.wait_ge(a_done, B + 1)
                with act.Fori(0, B // 2) as pair:
                    b0 = pair * 2
                    ln_scalar(act, x1, b0, b0 + B, ln_bank)

            @block.tensor
            def _(pe):
                pe.wait_ge(const_in, 7 * 16)
                pe.wait_ge(const_ready, 7)
                with pe.Fori(0, B // 2) as pair:
                    b0 = pair * 2
                    ln_tensor(pe, b0, ln_bank)
                pe.wait_ge(ln_done, B)

                def slot(t, parity, now, after):
                    prep, one, two = now
                    fills = fills_before(t)

                    def rows(par):
                        return slice(ROWS * par, ROWS * par + ROWS)

                    def scores(u, p):
                        one, two = (now[1:], after)[u]
                        par = (parity + u) % 2
                        if one:
                            g1, par1, j, es1 = unit(UNITS1, p)
                            w1 = 128 * (j + 1)
                            if p % (2 * NQ) == 0:
                                since(pe, tr_read, fills + (two + 4 if g1 else slot_fills))
                            since(pe, max_done, t * NU + (u * NU + NU + p - 1))
                        if two:
                            g2, par2, k, es2 = unit(UNITS2, p)
                            w2 = 128 * (T - k)
                            if p % (2 * NQ) == 0:
                                pe.wait_ge(mt_in, 64 * t + (64 * u + 32 * g2 + 32))
                            pe.wait_ge(p_ready, t * NU + (u * NU + p + 1))
                        alone(pe)
                        if one:
                            q, k_ = (qkT[rows(par1), 1 - par, i, :, :] for i in range(2))
                            for i, e in enumerate(es1):
                                nc.tensor.matmul(s1_psum[:, p % 2, w1 * i:w1 * i + w1], q[:, 4 * g1 + e, 128 * j:128 * j + 128],
                                                 k_[:, 4 * g1 + e, 0:w1], start=i == 0, stop=False)
                        if two:
                            q, k_ = (qkT[rows(par2), par, i, :, :] for i in range(2))
                            for i, e in enumerate(es2):
                                nc.tensor.matmul(s2_psum[:, p % 2, w2 * i:w2 * i + w2], k_[:, 4 * g2 + e, 128 * k:128 * k + 128],
                                                 q[:, 4 * g2 + e, 128 * k:S], start=i == 0, stop=False)
                        if one:
                            for i, e in enumerate(es1):
                                ins = nc.tensor.matmul(s1_psum[:, p % 2, w1 * i + w1 - 128:w1 * i + w1], ident_bf[:, :],
                                                       mask_bf[:, 0:128], start=False, stop=e == es1[-1])
                            ins.then_inc(s1_done, 1)
                        if two:
                            for i, e in enumerate(es2):
                                ins = nc.tensor.matmul(s2_psum[:, p % 2, w2 * i:w2 * i + 128], mask_bf[:, 0:128],
                                                       ident_bf[:, :], start=False, stop=e == es2[-1])
                            ins.then_inc(s2_done, 1)

                    def values(u, last):
                        quad, k = last // NQ, LAST[last % NQ]
                        g, par = quad // 2, (quad + 1) % 2
                        if quad == 0 and k == 0:
                            pe.wait_ge(a_v, t + (u + 1))
                        if k == 0:
                            pe.wait_ge(o_read, 4 * t + (4 * u + quad + 1))
                        pe.wait_ge(p_ready, t * NU + (u * NU + last + 3))
                        alone(pe)
                        for e in range(4):
                            ins = nc.tensor.matmul(o_psum[32 * e:32 * e + 32, quad % 2, 128 * k:S],
                                                   v_a[:, (parity + u) % 2, k, 8 * g + 2 * e + par, :], pT_a[k][:, e, :],
                                                   start=k == 0, stop=k == T - 1)
                        ins.then_inc(pv_a, 1)

                    def output(quad):
                        pe.wait_ge(o_read, 4 * t + quad + 3)
                        if quad == 0 and prep:
                            pe.wait_ge(a_qkv, 4 * (t + 3))
                        elif quad == 0:
                            pe.wait_ge(a_done, t + 1)
                        else:
                            pe.wait_ge(ao_ready, 4 * t + quad + 4)
                        alone(pe)
                        for j in range(T):
                            ins = nc.tensor.transpose(m_psum[:, 128 * j:128 * j + 128], o_a[:, quad % 2, 128 * j:128 * j + 128],
                                                      ident[:, :])
                        ins.then_inc(ot_a, 1)

                    def fill(at, n, g):
                        since(pe, tr_read, fills + at)
                        alone(pe)
                        pr = 4 * g + 2 * (n % 2)
                        for c in range(2):
                            for j in range(T):
                                r = HEADS * j + 2 * (pr + c)
                                ins = nc.tensor.transpose(tr_psum[:, c, 128 * j:128 * j + 128],
                                                          qk_st[:, n // 2, r:r + 2, :], ident_bf[:, :])
                        ins.then_inc(tr_done, 1)

                    def transpose_maxima(g):
                        since(pe, tr_read, fills + (0 if g else two + 4))
                        pe.wait_ge(mx_step, 10 * t + (10 if g else 15))
                        alone(pe)
                        for j in range(T):
                            ins = nc.tensor.transpose(tr_psum[0:24, 0, 128 * j:128 * j + 128], mx_st[:, j, :], ident_bf[:, :])
                        ins.then_inc(tr_done, 1)

                    def project(j):
                        if j == 0:
                            pe.wait_ge(a_x, t + 3)
                            since(pe, a_done, t + 1)
                        else:
                            pe.wait_ge(a_qkv, 4 * (t + 2) + j)
                        alone(pe)
                        nc.tensor.matmul(m_psum[:, 0:3 * D], xa[:, 128 * j:128 * j + 128], w_qkv_a[:, :],
                                         start=True, stop=True).then_inc(a_proj, 1)

                    slot_fills = two + 5 * one + 4 * prep
                    for P in range(HEAD_UNITS, NU + HEAD_UNITS):
                        u, p = P // NU, P % NU
                        if any((now[1:], after)[u]):
                            scores(u, p)
                        v, last = (P - 2) // NU, (P - 2) % NU
                        if (two, after[1])[v] and last % NQ in LAST:
                            values(v, last)
                        if prep and P in PROJ_AT:
                            project(PROJ_AT.index(P))
                        if two and P >= NQ + OUT_AT and P % NQ == OUT_AT:
                            output(P // NQ - 1)
                        if two and P == LAST_MAXIMA_AT:
                            transpose_maxima(1)
                        if one and P in FILL_AT:
                            n = FILL_AT.index(P)
                            fill(two + n, n, 1)
                        if one and P == MAXIMA_AT:
                            transpose_maxima(0)
                        if prep and P in LAST_FILL_AT:
                            n = LAST_FILL_AT.index(P)
                            if n == 0:
                                pe.wait_ge(parts_ready, 2 * t + 6)
                                pe.wait_ge(part1_ready, 6 * t + 18)
                                pe.wait_ge(part2_again, 2 * t + 6)
                            fill(two + 5 * one + n, n, 0)
                        if two and P == OUT_T_AT:
                            pe.wait_ge(ao_ready, 4 * t + 8)
                            alone(pe)
                            for j in range(T):
                                ins = nc.tensor.transpose(m_psum[:, 128 * j:128 * j + 128], ao_t[:, j, :], ident[:, :])
                            ins.then_inc(aot_done, 1)
                        if two and P == PROJ_OUT_AT:
                            pe.wait_ge(aot_read, t + 1)
                            alone(pe)
                            nc.tensor.matmul(m_psum[:, :], w_proj_a[:, :], ao_a[:, :], start=True, stop=True).then_inc(a_out, 1)

                slots(pe, slot)
                pe.wait_ge(a_done, B + 1)
                with pe.Fori(0, B // 2) as pair:
                    b0 = pair * 2
                    ln_tensor(pe, b0 + B, ln_bank)

            @block.vector
            def _(dve):
                dve.wait_ge(x_in, 16)
                dve.wait_ge(const_in, 7 * 16)
                dve.wait_ge(const_ready, 7)
                with dve.Fori(0, B // 2) as pair:
                    b0 = pair * 2
                    ln_vector(dve, xn, b0, b0, ln_bank)
                dve.sem_inc(a_done, 1)
                dve.sem_inc(ao_ready, 4)
                dve.sem_inc(o_read, 2)
                dve.sem_inc(ot_a, 2)
                dve.sem_inc(p_ready, 2)
                dve.sem_inc(pv_a, 4)

                def slot(t, parity, now, after):
                    prep, one, two = now

                    def maximum(u, p):
                        g, par, j, es = unit(UNITS1, p)
                        n, w = len(es), 128 * (j + 1)
                        dve.wait_ge(s1_done, t * NU + (u * NU + NU + p + 1))
                        if p % (2 * NQ) == 0:
                            since(dve, mx_step, 10 * t + (10 * u + 5 * g + 5))
                        alone(dve)
                        at = 4 * par + es[0]
                        dve.tensor_reduce(mx_a[:, g, j, at:at + n], s1_psum[:, p % 2, 0:n * w].rearrange("p (e w) -> p e w", w=w),
                                          AX.X, ALU.max).then_inc(max_done, 1)

                    def split_maxima(u, g, step):
                        n = 2 * t + 2 * u + g
                        m = mx_a[:, g, :, :].rearrange("p j (a e) -> p j a e", e=4)
                        rest4 = mx_rest[:, :, :].rearrange("p j (a e) -> p j a e", e=4)
                        parts = mx_st[:, :, :].rearrange("p j (a c e) -> p j a c e", a=2, c=3)
                        if step == 0:
                            if g == 0:
                                since(dve, tr_done, fills_before(t) + two)
                            elif not (isinstance(t, int) and t == -1):
                                dve.wait_ge(tr_done, fills_before(t) + two + 4 * one + 1)
                            else:
                                dve.wait_ge(tr_done, fills_before(t) + 5)
                            dve.wait_ge(max_done, t * NU + (u * NU + 2 * NQ * (g + 1)))
                        else:
                            dve.wait_ge(mx_step, 5 * n + step)
                        alone(dve)
                        if step % 2 == 0:
                            src = m if step == 0 else rest4
                            ins = dve.tensor_copy(parts[:, :, :, step // 2, :], src)
                        else:
                            src = m if step == 1 else rest4
                            ins = dve.tensor_tensor(rest4, src, parts[:, :, :, step // 2, :], ALU.subtract)
                        ins.then_inc(mx_step, 1)

                    def normalise(quad):
                        g, par = quad // 2, (quad + 1) % 2
                        dve.wait_ge(ot_a, 4 * t + quad + 3)
                        dve.wait_ge(ao_ready, 4 * t + quad + 4)
                        alone(dve)
                        o = m_psum[:, :].rearrange("p (j e d) -> p j e d", j=T, e=4)
                        dve.reciprocal(rs_a[:, :, :], o[:, :, :, HD]).then_inc(rs_ready, 1)
                        dve.wait_ge(rs_ready, 4 * t + quad + 1)
                        alone(dve)
                        dst = ao_t[:, :, 64 * g:64 * g + 64].rearrange("p j (e a d) -> p j e a d", a=2, d=HD)[:, :, :, par, :]
                        dve.tensor_tensor(dst, o[:, :, :, 0:HD], rs_a[:, :, :].unsqueeze(3).broadcast_to([128, T, 4, HD]),
                                          ALU.mult).then_inc(ao_ready, 1)

                    for P in range(HEAD_UNITS, NU + HEAD_UNITS):
                        u, p = P // NU, P % NU
                        if two and P > NQ + OUT_AT and P % NQ == OUT_AT + 1:
                            normalise(P // NQ - 1)
                        if (one, after[0])[u]:
                            maximum(u, p)
                        if after[1] and 0 <= P - NU - 1 < 5:
                            split_maxima(1, 1, P - NU - 1)
                        if one and 0 <= P - 2 * NQ < 5:
                            split_maxima(1, 0, P - 2 * NQ)
                        if prep and P in PROJ_AT:
                            j = PROJ_AT.index(P)
                            if j == 0:
                                since(dve, a_v, t + 2)
                            dve.wait_ge(a_proj, 4 * (t + 2) + j + 1)
                            alone(dve)
                            dve.tensor_tensor(qkv_a[:, j, :], m_psum[:, 0:3 * D], bias_a[:, :], ALU.add).then_inc(a_qkv, 1)
                        if prep and P == PART2_AT:
                            dve.wait_ge(part2_ready, 2 * t + 6)
                            alone(dve)
                            for i in range(2):
                                part = places(st_part(i, 1))
                                dve.tensor_copy(part[:, :, :, 1, :], part[:, :, :, 0, :]).then_inc(part2_again, 1)
                        if two and P == PROJ_OUT_AT:
                            dve.wait_ge(a_out, t + 1)
                            alone(dve)
                            dve.scalar_tensor_tensor(x1[:, t, :], m_psum[:, :], bias_proj[:, :], x1[:, t, :],
                                                     ALU.add, ALU.add).then_inc(a_done, 1)

                slots(dve, slot)
                with dve.Fori(0, B // 2) as pair:
                    b0 = pair * 2
                    ln_vector(dve, xres, b0, b0 + B, ln_bank)
        part.close()

        part = ExitStack()
        w_qkv = sb(part, "w_qkv", [128, 3 * INNER])
        w_qk_hi = sb(part, "w_qk_hi", [128, 2 * INNER], F32R)
        w_qk_lo = sb(part, "w_qk_lo", [128, 2 * INNER], F32R)
        w_o = sb(part, "w_o", [128, INNER // 128, D])
        w_1 = sb(part, "w_1", [128, 2 * FF])
        w_2 = sb(part, "w_2", [128, 3, D])
        vec = sb(part, "vec", [128, NVEC])
        scale_bc = sb(part, "scale_bc", [128, 4 * WD])
        rope = sb(part, "rope", [128, T, 4, WD])
        xs = sb(part, "xs", [128, WIN + S])
        xs_hi = sb(part, "xs_hi", [128, S], F32R)
        xs_lo = sb(part, "xs_lo", [128, S], F32R)
        raw = xn[:, 0:4, :].rearrange("p (k q) t -> p k q t", k=2)
        sq = xn[:, 4:8, :].rearrange("p (k g) (h d) -> p k (g h) d", k=2, d=WD)
        ss = sb(part, "ss", [128, 2, 2 * HALF])
        ssm = sb(part, "ssm", [128, 2 * HALF])
        rn = sb(part, "rn", [128, 2, 2 * HALF])
        power = sb(part, "power", [128, 2 * HALF])
        rota = sb(part, "rota", [128, 2, 2, HALF * WD])
        rotb = sb(part, "rotb", [128, 2, 2, HALF * WD])
        rots = sb(part, "rots", [128, 2, 2 * HALF, WD])
        qkn = sb(part, "qkn", [128, 2, 2, HALF * WD])
        v_t = sb(part, "v_t", [128, 4, T, HALF * WD // 2])
        qT = sb(part, "qT", [128, 2, 4, 128])
        kT = sb(part, "kT", [128, 8, WIN + S])
        pr = sb(part, "pr", [128, 2, HALF, WD])
        pe_ = sb(part, "pe_", [128, 2, HALF, WD])
        mx = sb(part, "mx", [128, 2, HALF])
        den = sb(part, "den", [128, 2, HALF])
        rden = sb(part, "rden", [128, 2, HALF])
        pT = sb(part, "pT", [128, 2, HALF * WD])
        o_t = sb(part, "o_t", [128, 2, HALF * WD])
        oT = sb(part, "oT", [128, 2, 4, 128])
        hid = rota[:, :, :, :].rearrange("p k q t -> p (k q) t")
        gel = rotb[:, :, 0, :]
        pj_psum = ps(part, "pj_psum", [128, 2, S])
        t_psum = ps(part, "t_psum", [128, S])
        s_psum = ps(part, "s_psum", [128, 2, S])
        ov_psum = ps(part, "ov_psum", [128, 2, S])
        ow_psum = ps(part, "ow_psum", [128, S])

        attn_w_in = sem("attn_w_in")
        ffn_w_in = sem("ffn_w_in")
        pad_zero = sem("pad_zero")
        rope_ready = sem("rope_ready")
        attn_done = sem("attn_done")
        ffn_done = sem("ffn_done")
        xs_ready = sem("xs_ready")
        w_hi_ready = sem("w_hi_ready")
        w_parts_ready = sem("w_parts_ready")
        xs_hi_ready = sem("xs_hi_ready")
        xs_parts_ready = sem("xs_parts_ready")
        proj_done = sem("proj_done")
        proj_read = sem("proj_read")
        sq_ready = sem("sq_ready")
        ss_ready = sem("ss_ready")
        ssm_ready = sem("ssm_ready")
        rn_ready = sem("rn_ready")
        rotb_ready = sem("rotb_ready")
        rots_ready = sem("rots_ready")
        qkn_ready = sem("qkn_ready")
        t_done = sem("t_done")
        t_read = sem("t_read")
        s_done = sem("s_done")
        mx_ready = sem("mx_ready")
        sub_ready = sem("sub_ready")
        exp_ready = sem("exp_ready")
        den_ready = sem("den_ready")
        rden_ready = sem("rden_ready")
        pt_done = sem("pt_done")
        pt_read = sem("pt_read")
        pv_done = sem("pv_done")
        o_ready = sem("o_ready")
        ot_done = sem("ot_done")
        ot_read = sem("ot_read")
        wo_done = sem("wo_done")
        up_done = sem("up_done")
        gel_ready = sem("gel_ready")
        hid_ready = sem("hid_ready")
        down_done = sem("down_done")
        fin = sem("fin")
        out_done = sem("out_done")

        ATT_IN = 4 * 16
        FFN_IN = 3 * 16
        HW = HALF * WD

        def up_bank(c, gate):
            return (pj_psum, s_psum)[c % 2][:, gate, :]

        ln_bank = [ov_psum[:, k, :] for k in range(2)]
        first_bank = [pj_psum[:, k, :] for k in range(2)]

        HEAD, BODY, TAIL = range(3)
        LAG = 4

        def runs(mode, st, lag):
            return st >= lag if mode == HEAD else st < lag if mode == TAIL else True

        def place(b, u, st, lag):
            back = st < lag
            return (b - 1, u - 1, st - lag + STEPS) if back else (b, u, st - lag)

        def stream(engine, l, step):
            for st in range(STEPS):
                step(HEAD, 0, l * B, st)
            with engine.Fori(1, B) as b:
                for st in range(STEPS):
                    step(BODY, b, l * B + b, st)
            for st in range(LAG):
                step(TAIL, B, l * B + B, st)

        with nc.Block() as block:
            @block.sync
            def _(sp):
                with sp.Fori(0, LAYERS) as l:
                    sp.wait_ge(attn_done, l * (B * T) + 1)
                    sp.dma_start(w_qkv[:, :], wqkv[l, :, :]).then_inc(attn_w_in, 16)
                    sp.dma_start(rope[:, :, :, :].rearrange("p j f d -> p j (f d)"), win_rope).then_inc(attn_w_in, 16)
                    sp.dma_start(w_o[:, :, :], wo[l, :, :, :]).then_inc(attn_w_in, 16)
                    sp.dma_start(scale_bc[:, :], qk_scale[l, :].partition_broadcast(128)).then_inc(attn_w_in, 16)
                    sp.wait_ge(ffn_done, l * B + B)
                    sp.dma_start(vec[:, :], vecs[l, :, :]).then_inc(ffn_w_in, 16)
                    sp.dma_start(w_1[:, :], w1[l, :, :]).then_inc(ffn_w_in, 16)
                    sp.dma_start(w_2[:, :, :], w2[l, :, :, :]).then_inc(ffn_w_in, 16)
                with sp.Fori(0, B) as b:
                    sp.wait_ge(fin, b + 1)
                    sp.dma_start(outT[:, b, :], x1[:, b, :]).then_inc(out_done, 16)
                sp.wait_ge(out_done, 16 * B)

            @block.gpsimd
            def _(pool):
                pool.memset(power[:, :], -0.5).then_inc(pad_zero, 1)
                pool.memset(xs[:, 0:WIN + 1], 0.0).then_inc(pad_zero, 1)
                pool.memset(kT[:, :, 0:WIN], 0.0).then_inc(pad_zero, 1)
                pool.memset(ln_x[:, :, 0:1], 0.0).then_inc(pad_zero, 1)
                pool.memset(xres[:, B, :], 0.0).then_inc(pad_zero, 1)
                pool.wait_ge(pad_zero, 5)
                with pool.Fori(0, LAYERS) as l:
                    pool.wait_ge(attn_w_in, l * ATT_IN + ATT_IN)
                    r = rope[:, :, :, :].rearrange("p j f d -> p j (f d)")
                    pool.tensor_tensor(r, r, scale_bc[:, :].unsqueeze(1).broadcast_to([128, T, 4 * WD]), ALU.mult).then_inc(rope_ready, 1)
                    pool.tensor_copy(w_qk_hi[:, :], w_qkv[:, 0:2 * INNER]).then_inc(w_hi_ready, 1)
                    pool.wait_ge(w_hi_ready, l + 1)
                    alone(pool)
                    pool.tensor_tensor(w_qk_lo[:, :], w_qkv[:, 0:2 * INNER], w_qk_hi[:, :], ALU.subtract).then_inc(w_parts_ready, 1)

                    def split_xs(n, j):
                        x = xs[:, WIN + 128 * j:WIN + 128 * j + 128]
                        hi, lo = (t[:, 128 * j:128 * j + 128] for t in (xs_hi, xs_lo))
                        pool.wait_ge(xs_ready, n + 1)
                        alone(pool)
                        pool.tensor_copy(hi, x).then_inc(xs_hi_ready, 1)
                        pool.wait_ge(xs_hi_ready, n + 1)
                        alone(pool)
                        pool.tensor_tensor(lo, x, hi, ALU.subtract).then_inc(xs_parts_ready, 1)

                    split_xs(l * (B * T + 2), 0)
                    split_xs(l * (B * T + 2) + 1, 1)
                    with pool.Fori(0, B) as b:
                        base = (l * B + b) * STEPS
                        for i in range(STEPS):
                            n = base + i
                            k = i % 2
                            if i % 2:
                                split_xs(l * (B * T + 2) + b * T + (2 + i // 2), (2 + i // 2) % T)
                            pool.wait_ge(rotb_ready, 2 * n + 2)
                            pool.tensor_tensor(flat(rots[:, k, :, :]), flat(rota[:, k, :, :]), flat(rotb[:, k, :, :]),
                                               ALU.add).then_inc(rots_ready, 1)
                            pool.wait_ge(ss_ready, n + 1)
                            alone(pool)
                            pool.tensor_scalar(ssm[:, :], ss[:, k, :], 1e-24, None, ALU.max).then_inc(ssm_ready, 1)
                            pool.wait_ge(ssm_ready, n + 1)
                            pool.tensor_tensor(rn[:, k, :], ssm[:, :], power[:, :], ALU.pow).then_inc(rn_ready, 1)

            @block.scalar
            def _(act):
                act.wait_ge(pad_zero, 5)
                act.sem_inc(proj_read, 2)
                act.wait_ge(ln_done, 2 * B)

                def copy_proj(base, i, q):
                    act.wait_ge(proj_done, 4 * (base + i) + q + 1)
                    dst = raw[:, i % 2, q, :] if q < 2 else flat(v_t[:, i % 4, 2 * q - 4:2 * q - 2, :])
                    act.activation(dst, pj_psum[:, q % 2, :], ACT.Copy).then_inc(proj_read, 1)

                def squares(base, i):
                    n = base + i
                    act.wait_ge(proj_read, 4 * n + 4)
                    act.activation(flat(sq[:, i % 2, :, :]), flat(raw[:, i % 2, :, :]), ACT.Square).then_inc(sq_ready, 1)

                def copy_t(base, i, q):
                    j, g = i // 2, i % 2
                    act.wait_ge(t_done, 2 * (base + i) + q + 1)
                    if q == 0:
                        dst, src = qT[:, i % 2, :, :], t_psum[:, :].rearrange("p (c t) -> p c t", c=4)
                    else:
                        dst = kT[:, 4 * g:4 * g + 4, WIN + 128 * j:WIN + 128 * j + 128].rearrange("p (r c) t -> p r c t", r=2)
                        src = s_psum[:, :, 256:S].rearrange("p r (c t) -> p r c t", c=2)
                    act.activation(dst, src, ACT.Copy).then_inc(t_read, 1)

                def exponentials(base, i):
                    act.wait_ge(sub_ready, base + i + 1)
                    act.activation(flat(pe_[:, i % 2, :, :]), flat(pr[:, i % 2, :, :]), ACT.Exp).then_inc(exp_ready, 1)

                def copy_pt(base, i):
                    act.wait_ge(pt_done, base + i + 1)
                    act.activation(pT[:, i % 2, :], t_psum[:, :], ACT.Copy).then_inc(pt_read, 1)

                def copy_ot(base, i):
                    act.wait_ge(ot_done, base + i + 1)
                    act.activation(oT[:, i % 2, :, :].rearrange("p (r c) t -> p r (c t)", r=2), ov_psum[:, :, 256:S], ACT.Copy).then_inc(ot_read, 1)

                def copy_xs(b, j):
                    to = WIN + 128 * j
                    lo = 0 if j else 1
                    act.activation(xs[0:64, to:to + 128], xres[0:64, b, 128 * j:128 * j + 128], ACT.Copy)
                    act.activation(xs[64:128, to + lo:to + 128], xres[64:128, b, 128 * j + lo - 1:128 * j + 127],
                                   ACT.Copy).then_inc(xs_ready, 1)

                def step(mode, b, u, st):
                    def run(stage, lag, *more):
                        if runs(mode, st, lag):
                            _, v, i = place(b, u, st, lag)
                            stage(v * STEPS, i, *more)
                    if mode == TAIL and st == 0:
                        act.wait_ge(attn_done, u * T - (B - 2) * T + 1)
                        alone(act)
                        ln_copy(act, xres, 0, True)
                    if mode == TAIL and st == 1:
                        ln_root(act, u + B, first_bank)
                    run(copy_proj, 0, 0)
                    run(exponentials, 2)
                    run(copy_proj, 0, 1)
                    run(copy_ot, 3)
                    run(copy_pt, 2)
                    run(copy_proj, 0, 2)
                    run(copy_proj, 0, 3)
                    run(squares, 0)
                    if mode == TAIL and st == 0:
                        ln_square(act, u + B)
                    run(copy_t, 1, 0)
                    run(copy_t, 1, 1)
                    if mode != TAIL and st % 2 == 0:
                        copy_xs(b + st // 4, (2 + st // 2) % T)

                copy_xs(0, 0)
                copy_xs(0, 1)
                with act.Fori(0, LAYERS) as l:
                    act.wait_ge(ffn_done, l * B + B)
                    alone(act)
                    stream(act, l, step)
                    act.wait_ge(attn_done, (l + 1) * (B * T) + 1)
                    alone(act)

                    def gates(b):
                        u = l * B + b
                        for c in range(3):
                            act.wait_ge(up_done, (u * 3 + c) * 2 + 2)
                            if c == 2:
                                act.wait_ge(hid_ready, u * 3 + 1)
                            m = FC[c]
                            act.activation(gel[0:m, c % 2, :], up_bank(c, 1)[0:m, :], ACT.Gelu,
                                           bias=vec[0:m, 6 + c:7 + c]).then_inc(gel_ready, 1)

                    v = (l + 2) * B
                    with act.Fori(0, B // 2 - 1) as pair:
                        b0 = pair * 2
                        ln_copy(act, xres, b0 + 2, True)
                        gates(b0)
                        ln_square(act, v + b0 + 2)
                        ln_root(act, v + b0 + 2, ln_bank)
                        gates(b0 + 1)
                    gates(B - 2)
                    act.wait_ge(ffn_done, l * B + B + 1)
                    alone(act)
                    copy_xs(0, 0)
                    copy_xs(0, 1)
                    gates(B - 1)

            @block.tensor
            def _(pe):
                pe.wait_ge(pad_zero, 5)
                pe.wait_ge(ln_done, 2 * B)

                def proj(base, i, q):
                    j, g = i // 2, i % 2
                    col = min(q, 2) * INNER + g * HW
                    pe.wait_ge(proj_read, 4 * (base + i) + q + 1)
                    if q < 2:
                        hi, lo = (t[:, 128 * j:128 * j + 128] for t in (xs_hi, xs_lo))
                        w_hi, w_lo = (t[:, col:col + HW] for t in (w_qk_hi, w_qk_lo))
                        nc.tensor.matmul(pj_psum[:, q, :], hi, w_hi, start=True, stop=False)
                        nc.tensor.matmul(pj_psum[:, q, :], hi, w_lo, start=False, stop=False)
                        ins = nc.tensor.matmul(pj_psum[:, q, :], lo, w_hi, start=False, stop=True)
                    else:
                        for w in (2 * q - 4, 2 * q - 3):
                            at = 128 * j + WIN * w
                            for par in range(2):
                                cols = w_qkv[:, col:col + HW].rearrange("p (c r d) -> p r c d", r=2, d=WD)[:, par, :, :]
                                to = 256 * (w % 2)
                                ins = nc.tensor.matmul(pj_psum[64 * par:64 * par + 64, q % 2, to:to + 256],
                                                       xs[:, at:at + 64], cols, start=True, stop=True)
                    ins.then_inc(proj_done, 1)

                def t_qk(base, i):
                    n = base + i
                    pe.wait_ge(qkn_ready, n + 1)
                    for q in range(2):
                        for c in range(4):
                            to = s_psum[:, c // 2, 256 + 128 * (c % 2):384 + 128 * (c % 2)] if q else t_psum[:, 128 * c:128 * c + 128]
                            ins = nc.tensor.transpose(to, qkn[:, i % 2, q, 128 * c:128 * c + 128], ident[:, :])
                        ins.then_inc(t_done, 1)

                def scores(base, i):
                    j, g = i // 2, i % 2
                    pe.wait_ge(t_read, 2 * (base + i) + 2)
                    first = 128 + (0 if j == 0 else 256)
                    for par in range(2):
                        nc.tensor.matmul(s_psum[:, par, 0:256], ident_bf[:, :], mask_bf[:, first:first + 256],
                                         start=True, stop=False)
                    for par in range(2):
                        r = slice(64 * par, 64 * par + 64)
                        for c in range(4):
                            for w in range(4):
                                ins = nc.tensor.matmul(s_psum[32 * w:32 * w + 32, par, 64 * c:64 * c + 64],
                                                       qT[r, i % 2, c, 32 * w:32 * w + 32],
                                                       kT[r, 4 * g + c, 128 * j + 32 * w:128 * j + 32 * w + 64],
                                                       start=False, stop=c == 3)
                    ins.then_inc(s_done, 1)

                def t_p(base, i):
                    pe.wait_ge(exp_ready, base + i + 1)
                    for c in range(4):
                        ins = nc.tensor.transpose(t_psum[:, 128 * c:128 * c + 128],
                                                  flat(pe_[:, i % 2, 2 * c:2 * c + 2, :]), ident[:, :])
                    ins.then_inc(pt_done, 1)

                def values(base, i, par):
                    n = base + i
                    pe.wait_ge(pt_read, n + 1)
                    pe.wait_ge(proj_read, 4 * n + 6)
                    pe.wait_ge(ot_read, n + 1)
                    alone(pe)
                    r = slice(64 * par, 64 * par + 64)
                    for c in range(4):
                        for w in range(4):
                            ins = nc.tensor.matmul(ov_psum[32 * w:32 * w + 32, par, 64 * c:64 * c + 64],
                                                   pT[r, i % 2, 128 * c + 32 * w:128 * c + 32 * w + 32],
                                                   v_t[r, i % 4, w, 64 * c:64 * c + 64], start=True, stop=True)
                    if par:
                        ins.then_inc(pv_done, 1)

                def t_o(base, i):
                    pe.wait_ge(o_ready, base + i + 1)
                    for c in range(4):
                        ins = nc.tensor.transpose(ov_psum[:, c // 2, 256 + 128 * (c % 2):384 + 128 * (c % 2)],
                                                  o_t[:, i % 2, 128 * c:128 * c + 128], ident[:, :])
                    ins.then_inc(ot_done, 1)

                def out_proj(u, i):
                    pe.wait_ge(ot_read, u * STEPS + i + 2)
                    if i % 2 == 0:
                        pe.wait_ge(attn_done, u * T + i // 2 + 1)
                    for c in range(4):
                        ins = nc.tensor.matmul(ow_psum[:, 0:128], w_o[:, 4 * (i % 2) + c, :], oT[:, i % 2, c, :],
                                               start=i % 2 == 0 and c == 0, stop=i % 2 == 1 and c == 3)
                    if i % 2:
                        ins.then_inc(wo_done, 1)

                with pe.Fori(0, LAYERS) as l:
                    pe.wait_ge(attn_w_in, l * ATT_IN + ATT_IN)
                    pe.wait_ge(w_parts_ready, l + 1)
                    alone(pe)

                    def step(mode, b, u, st):
                        def run(stage, lag, *more):
                            if runs(mode, st, lag):
                                _, v, i = place(b, u, st, lag)
                                stage(v * STEPS, i, *more)
                        if mode != TAIL and st % 2 == 0:
                            pe.wait_ge(xs_parts_ready, l * (B * T + 2) + b * T + st // 2 + 1)
                        run(proj, 0, 0)
                        run(proj, 0, 1)
                        run(t_o, 3)
                        if mode == TAIL and st == 0:
                            ln_mean(pe, u + B, first_bank)
                        run(proj, 0, 2)
                        run(t_p, 2)
                        run(proj, 0, 3)
                        run(values, 2, 0)
                        run(values, 2, 1)
                        run(t_qk, 1)
                        if runs(mode, st, 3):
                            _, v, i = place(b, u, st, 3)
                            out_proj(v, i)
                        run(scores, 1)
                        if mode == TAIL and st == 0:
                            ln_variance(pe, u + B, first_bank)

                    stream(pe, l, step)
                    pe.wait_ge(ffn_w_in, l * FFN_IN + FFN_IN)
                    alone(pe)

                    def feed_forward(b):
                        u = l * B + b
                        for c in range(3):
                            if c == 0:
                                pe.wait_ge(ln_done, (l + 2) * B + b + 1)
                            if c == 2:
                                pe.wait_ge(hid_ready, u * 3 + 1)
                            for gate in range(2):
                                at = gate * FF + 128 * c
                                nc.tensor.matmul(up_bank(c, gate)[0:FC[c], :], w_1[:, at:at + FC[c]], xn[:, b, :],
                                                 start=True, stop=True).then_inc(up_done, 1)
                        pe.wait_ge(ffn_done, u + B)
                        for c in range(3):
                            pe.wait_ge(hid_ready, u * 3 + c + 1)
                            ins = nc.tensor.matmul(ow_psum[:, :], w_2[0:FC[c], c, :], hid[0:FC[c], c, :],
                                                   start=c == 0, stop=c == 2)
                        ins.then_inc(down_done, 1)

                    v = (l + 2) * B
                    with pe.Fori(0, B // 2 - 1) as pair:
                        b0 = pair * 2
                        ln_mean(pe, v + b0 + 2, ln_bank)
                        feed_forward(b0)
                        ln_variance(pe, v + b0 + 2, ln_bank)
                        feed_forward(b0 + 1)
                    feed_forward(B - 2)
                    feed_forward(B - 1)

            @block.vector
            def _(dve):
                dve.wait_ge(pad_zero, 5)
                dve.wait_ge(ln_done, 2 * B)
                dve.sem_inc(attn_done, 1)
                dve.sem_inc(ot_read, 1)
                dve.sem_inc(ffn_done, B)

                def heads(ap):
                    return ap.rearrange("p (h d) -> p h d", d=WD)

                def rotate(base, i, own):
                    k, j, half = i % 2, i // 2, WD // 2
                    x = raw[:, k, :, :].rearrange("p q (h d) -> p q h d", d=WD)
                    y = rotb[:, k, :, :].rearrange("p q (h d) -> p q h d", d=WD)

                    def table(f, lo, hi):
                        t = rope[:, j, :, :].rearrange("p (q f) d -> p q f d", f=2)[:, :, f, lo:hi]
                        return t.unsqueeze(2).broadcast_to([128, 2, HALF, hi - lo])

                    if own:
                        dve.wait_ge(proj_read, 4 * (base + i) + 4)
                        dve.tensor_tensor(rota[:, k, :, :].rearrange("p q (h d) -> p q h d", d=WD), x, table(0, 0, WD), ALU.mult)
                        return
                    dve.tensor_tensor(y[:, :, :, 0:half], x[:, :, :, half:WD], table(1, half, WD), ALU.mult).then_inc(rotb_ready, 1)
                    dve.tensor_tensor(y[:, :, :, half:WD], x[:, :, :, 0:half], table(1, 0, half), ALU.mult).then_inc(rotb_ready, 1)

                def sum_squares(base, i):
                    dve.wait_ge(sq_ready, base + i + 1)
                    dve.tensor_reduce(ss[:, i % 2, :], sq[:, i % 2, :, :], AX.X, ALU.add).then_inc(ss_ready, 1)

                def subtract_max(base, i):
                    n, k = base + i, i % 2
                    s = s_psum[:, :, 0:256].rearrange("p r (c d) -> p r c d", d=WD)
                    dve.wait_ge(s_done, n + 1)
                    dve.tensor_reduce(mx[:, k, :].rearrange("p (r c) -> p r c", r=2), s, AX.X, ALU.max).then_inc(mx_ready, 1)
                    dve.wait_ge(mx_ready, n + 1)
                    dve.tensor_tensor(pr[:, k, :, :].rearrange("p (c r) d -> p r c d", r=2), s,
                                      mx[:, k, :].rearrange("p (r c) -> p r c", r=2).unsqueeze(3).broadcast_to([128, 2, 4, WD]),
                                      ALU.subtract).then_inc(sub_ready, 1)

                def normalise_qk(base, i):
                    n, k = base + i, i % 2
                    dve.wait_ge(rots_ready, n + 1)
                    dve.wait_ge(rn_ready, n + 1)
                    dve.tensor_tensor(flat(qkn[:, k, :, :]).rearrange("p (h d) -> p h d", d=WD), rots[:, k, :, :],
                                      rn[:, k, :].unsqueeze(2).broadcast_to([128, 2 * HALF, WD]), ALU.mult).then_inc(qkn_ready, 1)

                def sums(base, i):
                    n, k = base + i, i % 2
                    dve.wait_ge(exp_ready, n + 1)
                    dve.tensor_reduce(den[:, k, :], pe_[:, k, :, :], AX.X, ALU.add).then_inc(den_ready, 1)
                    dve.wait_ge(den_ready, n + 1)
                    dve.reciprocal(rden[:, k, :], den[:, k, :]).then_inc(rden_ready, 1)

                def outputs(base, i):
                    n, k = base + i, i % 2
                    dve.wait_ge(pv_done, n + 1)
                    dve.wait_ge(rden_ready, n + 1)
                    dve.tensor_tensor(o_t[:, k, :].rearrange("p (c r d) -> p r c d", r=2, d=WD),
                                      ov_psum[:, :, 0:256].rearrange("p r (c d) -> p r c d", d=WD),
                                      rden[:, k, :].rearrange("p (c r) -> p r c", r=2).unsqueeze(3).broadcast_to([128, 2, 4, WD]),
                                      ALU.mult).then_inc(o_ready, 1)

                with dve.Fori(0, LAYERS) as l:
                    dve.wait_ge(rope_ready, l + 1)
                    dve.wait_ge(ffn_done, l * B + B)
                    alone(dve)

                    def residual(u, b, i):
                        if i % 2:
                            j = i // 2
                            dve.wait_ge(wo_done, u * T + j + 1)
                            x = xres[:, b, 128 * j:128 * j + 128]
                            dve.tensor_tensor(x, x, ow_psum[:, 0:128], ALU.add).then_inc(attn_done, 1)

                    def step(mode, b, u, st):
                        def run(stage, lag, *more):
                            if runs(mode, st, lag):
                                _, v, i = place(b, u, st, lag)
                                stage(v * STEPS, i, *more)
                        run(subtract_max, 2)
                        run(sums, 2)
                        if runs(mode, st, 4):
                            c, v, i = place(b, u, st, 4)
                            residual(v, c, i)
                        if mode == TAIL and st == 0:
                            ln_center(dve, u + B, first_bank)
                        run(rotate, 0, True)
                        run(normalise_qk, 1)
                        run(rotate, 0, False)
                        if mode == TAIL and st == 1:
                            ln_reciprocal(dve, u + B, 0)
                        run(outputs, 2)
                        run(sum_squares, 0)
                        if mode == TAIL and st == 1:
                            ln_reciprocal(dve, u + B, 1)

                    stream(dve, l, step)
                    dve.wait_ge(ffn_w_in, l * FFN_IN + FFN_IN)
                    dve.wait_ge(attn_done, (l + 1) * (B * T) + 1)
                    alone(dve)

                    def hidden(b, chunks):
                        u = l * B + b
                        for c in chunks:
                            m = FC[c]
                            dve.wait_ge(gel_ready, u * 3 + c + 1)
                            dve.scalar_tensor_tensor(hid[0:m, c, :], up_bank(c, 0)[0:m, :], vec[0:m, 3 + c:4 + c],
                                                     gel[0:m, c % 2, :], ALU.add, ALU.mult).then_inc(hid_ready, 1)

                    def down_residual(b):
                        dve.wait_ge(down_done, l * B + b + 1)
                        dve.scalar_tensor_tensor(xres[:, b, :], ow_psum[:, :], vec[:, 2:3], xres[:, b, :],
                                                 ALU.add, ALU.add).then_inc(ffn_done, 1)

                    v = (l + 2) * B
                    gain, bias = vec[:, 0:1], vec[:, 1:2]
                    ln_finish(dve, xn, 0, v, gain, bias)
                    with dve.Fori(0, B // 2 - 1) as pair:
                        b0 = pair * 2
                        ln_center(dve, v + b0 + 2, ln_bank)
                        hidden(b0, (0, 1, 2))
                        down_residual(b0)
                        ln_reciprocal(dve, v + b0 + 2, 0)
                        hidden(b0 + 1, (0,))
                        ln_reciprocal(dve, v + b0 + 2, 1)
                        hidden(b0 + 1, (1, 2))
                        ln_finish(dve, xn, b0 + 2, v + b0 + 2, gain, bias)
                        down_residual(b0 + 1)
                    for b in (B - 2, B - 1):
                        hidden(b, (0, 1, 2))
                        down_residual(b)
                dve.wait_ge(ffn_done, LAYERS * B + B)
                with dve.Fori(0, B) as b:
                    dve.tensor_tensor(x1[:, b, :], x1[:, b, :], xres[:, b, :], ALU.add).then_inc(fin, 1)
        part.close()


def rotation_tables():
    f = np.float32
    half = HD // 2
    freqs = f(1.0) / f(10000.0) ** (np.arange(half, dtype=f) / f(half))
    ang = np.arange(S, dtype=f)[:, None] * freqs[None, :]
    a = np.stack([np.concatenate([np.cos(ang), np.cos(ang)], -1), np.concatenate([np.sin(ang), -np.sin(ang)], -1)], 1)
    a_rope = a.reshape(T, 128, 2, HD).transpose(1, 0, 2, 3)
    hf = np.arange(0, WD, 2, dtype=f)
    inv = f(1.0) / f(10000.0) ** (hf / f(WD))
    t = np.arange(S, dtype=f)
    ang = t[:, None] * inv[None, :]
    base = (hf + f(0.4 * WD)) / f(1.4 * WD)
    scale = base[None, :] ** ((t - f(S // 2)) / f(WIN // 2))[:, None]
    c, s = np.cos(ang), np.sin(ang)
    rows = []
    for k in (scale * f(QK_SCALE), f(1.0) / scale):
        rows += [np.concatenate([c * k, c * k], -1), np.concatenate([s * k, -s * k], -1)]
    win = np.stack(rows, 1).reshape(T, 128, 4 * WD).transpose(1, 0, 2)
    return np.ascontiguousarray(a_rope, f), np.ascontiguousarray(win, f)


def mask_tables():
    q = np.arange(128)
    causal = np.where(q[None, :] > q[:, None], MASKED, 0.0)
    r, k = (q % WIN)[:, None], np.arange(2 * WIN)[None, :]
    ok = np.where(k < WIN, k >= r, k - WIN <= r)
    first = ok & ~((q[:, None] < WIN) & (k < WIN))
    w = [np.tile(np.where(m, 0.0, MASKED), (1, 4)) for m in (first, ok)]
    return np.concatenate([causal] + w, 1).astype(np.float32)


def kernel(**inputs):
    import concourse.bacc as bacc
    from concourse.bass_utils import run_bass_kernel_spmd as run

    a = {k.replace("L0_", ""): np.asarray(v) for k, v in inputs.items()}
    a_rope, win_rope = rotation_tables()
    qs, ks = a["ffn_q_scale"], a["ffn_k_scale"]

    def columns(v):
        return np.pad(v, ((0, 0), (0, 384 - FF))).reshape(LAYERS, 3, 128).transpose(0, 2, 1)

    cols = [a["ffn_ln_g"][:, :, None], a["ffn_ln_b"][:, :, None], a["ffn_b2"][:, :, None],
            columns(a["ffn_b1"][:, :FF]), columns(a["ffn_b1"][:, FF:])]
    arrays = {
        "x_t": a["attn_x"].transpose(2, 0, 1),
        "a_w_t": a["attn_qkv_w"].T, "a_b": a["attn_qkv_b"],
        "a_proj_t": a["attn_proj_w"].T, "a_proj_b": a["attn_proj_b"][:, None],
        "a_rope": a_rope, "win_rope": win_rope, "masks": mask_tables(), "identity": np.eye(128, dtype=np.float32),
        "w_qkv": a["ffn_Wqkv"],
        "w_o": a["ffn_Wo"].reshape(LAYERS, INNER // 128, 128, D).transpose(0, 2, 1, 3),
        "w_1": a["ffn_W1"],
        "w_2": np.pad(a["ffn_W2"], ((0, 0), (0, 384 - FF), (0, 0))).reshape(LAYERS, 3, 128, D).transpose(0, 2, 1, 3),
        "vecs": np.concatenate(cols, 2),
        "qk_scale": np.concatenate([qs, qs, ks, ks], 1),
    }
    nc = bacc.Bacc("TRN2", target_bir_lowering=False, num_devices=1)
    feed, args = {}, []
    for name, v in arrays.items():
        feed[name] = np.ascontiguousarray(v)
        args.append(nc.dram_tensor("in_" + name, feed[name].shape, mybir.dt.from_np(feed[name].dtype), kind="ExternalInput").ap())
    out = nc.dram_tensor("out_t", (D, B, S), F32, kind="ExternalOutput").ap()
    program(nc, *args, out)
    r = run(nc, [{"in_" + k: v for k, v in feed.items()}], core_ids=[0])
    return np.ascontiguousarray(r.results[0]["out_t"].transpose(1, 2, 0))
```
